# Optimizing a Trainium2 kernel written in Bass

```python
import numpy as np
import jax
import jax.numpy as jnp

def _softmax(x, axis=-1):
    return jax.nn.softmax(x, axis=axis)

def _gelu(x):
    return jax.nn.gelu(x, approximate=True)

def _silu(x):
    return jax.nn.silu(x)

def _sigmoid(x):
    return jax.nn.sigmoid(x)

def _layernorm(x, axis=-1, eps=1e-05):
    m = jnp.mean(x, axis=axis, keepdims=True)
    v = jnp.var(x, axis=axis, keepdims=True)
    return (x - m) / jnp.sqrt(v + eps)

def _scatter_add(tgt, idx, src, axis=0):
    return tgt.at[idx].add(src)

def _segment_sum(src, seg, n):
    return jax.ops.segment_sum(src, seg, n)
kernel_name = 'mk_gnn_preln_d1_gnn_r8_ce48a6'

def setup_inputs(seed: int=0):
    np.random.seed(seed)
    _w = jnp.asarray

    def _rec_inputs():
        import jax
        import jax.numpy as jnp
        _gk = jax.random.key(seed)
        x = -0.000202 + 1 * jax.random.normal(jax.random.fold_in(_gk, 1), (12500, 128), jnp.float32)
        src = jax.random.randint(jax.random.fold_in(_gk, 2), (400000,), 0, 12500, jnp.int32)
        dst = jax.random.randint(jax.random.fold_in(_gk, 3), (400000,), 0, 12500, jnp.int32)
        _o = jnp.argsort(dst, stable=True)
        src = src[_o]
        dst = dst[_o]
        edge_attr_32 = 0.000196303 + 1.00016 * jax.random.normal(jax.random.fold_in(_gk, 11), (400000, 32), jnp.float32)
        return (x, src, dst, edge_attr_32)
    x, src, dst, edge_attr_32 = _rec_inputs()

    def _L0_gnn_setup():
        import jax, jax.numpy as jnp
        import numpy as np
        N, E = (6250, 100000)
        ND, ED, OD = (128, 32, 128)
        key = jax.random.key(seed)
        ks = jax.random.split(key, 12)
        inp = {'x': jax.random.normal(ks[0], (N, ND), dtype=jnp.float32), 'ei': jax.random.randint(ks[1], (2, E), 0, N, dtype=jnp.int64), 'ea': jax.random.normal(ks[2], (E, ED), dtype=jnp.float32), 'w1': jax.random.normal(ks[3], (2 * ND + ED, OD), dtype=jnp.float32) / np.sqrt(2 * ND + ED), 'b1': jnp.zeros((OD,), dtype=jnp.float32), 'w2': jax.random.normal(ks[4], (OD, OD), dtype=jnp.float32) / np.sqrt(OD), 'b2': jnp.zeros((OD,), dtype=jnp.float32), 'w_ih': jax.random.normal(ks[5], (OD, 3 * ND), dtype=jnp.float32) / np.sqrt(OD), 'b_ih': jnp.zeros((3 * ND,), dtype=jnp.float32), 'w_hh': jax.random.normal(ks[6], (ND, 3 * ND), dtype=jnp.float32) / np.sqrt(ND), 'b_hh': jnp.zeros((3 * ND,), dtype=jnp.float32)}
        return inp
    _L0_gnn_all = _L0_gnn_setup()
    _L0_gnn_in = {k: v for k, v in _L0_gnn_all.items() if k in ('w1', 'b1', 'w2', 'b2', 'w_ih', 'b_ih', 'w_hh', 'b_hh')}
    del _L0_gnn_all
    return {'x': x, 'src': src, 'dst': dst, 'edge_attr_32': edge_attr_32, 'L0_gnn_w1': _L0_gnn_in['w1'], 'L0_gnn_b1': _L0_gnn_in['b1'], 'L0_gnn_w2': _L0_gnn_in['w2'], 'L0_gnn_b2': _L0_gnn_in['b2'], 'L0_gnn_w_ih': _L0_gnn_in['w_ih'], 'L0_gnn_b_ih': _L0_gnn_in['b_ih'], 'L0_gnn_w_hh': _L0_gnn_in['w_hh'], 'L0_gnn_b_hh': _L0_gnn_in['b_hh']}

def reference(x, src, dst, edge_attr_32, L0_gnn_w1, L0_gnn_b1, L0_gnn_w2, L0_gnn_b2, L0_gnn_w_ih, L0_gnn_b_ih, L0_gnn_w_hh, L0_gnn_b_hh):
    import jax
    import jax.numpy as jnp

    def _L0_gnn_ref(x, ei, ea, w1, b1, w2, b2, w_ih, b_ih, w_hh, b_hh):
        import jax, jax.numpy as jnp
        import numpy as np
        N, E = (6250, 100000)
        ND, ED, OD = (128, 32, 128)
        s, d = (ei[0], ei[1])
        h = jnp.concatenate([x[s], x[d], ea], axis=-1)
        m = jax.nn.relu(h @ w1 + b1) @ w2 + b2
        agg = jax.ops.segment_sum(m, d, num_segments=x.shape[0])
        gi = agg @ w_ih + b_ih
        gh = x @ w_hh + b_hh
        i_r, i_z, i_n = jnp.split(gi, 3, axis=-1)
        h_r, h_z, h_n = jnp.split(gh, 3, axis=-1)
        r = jax.nn.sigmoid(i_r + h_r)
        z = jax.nn.sigmoid(i_z + h_z)
        n = jnp.tanh(i_n + r * h_n)
        return (1.0 - z) * n + z * x
    edge_index = jnp.stack([src, dst])
    h = jnp.maximum(_layernorm(x, axis=-1), 0.0)
    x = x + _L0_gnn_ref(h, edge_index, edge_attr_32, L0_gnn_w1, L0_gnn_b1, L0_gnn_w2, L0_gnn_b2, L0_gnn_w_ih, L0_gnn_b_ih, L0_gnn_w_hh, L0_gnn_b_hh)
    return x

_drawn_inputs = setup_inputs


def setup_inputs(seed=0):
    import zlib

    import numpy as np

    out = dict(_drawn_inputs(seed))
    spreads = {'L0_gnn_b1': (0.0, 0.1),
     'L0_gnn_b2': (0.0, 0.1),
     'L0_gnn_b_ih': (0.0, 0.766),
     'L0_gnn_b_hh': (0.0, 0.8)}
    factors = {}
    for name, (base, spread) in spreads.items():
        noise = np.random.default_rng([zlib.crc32(name.encode()), seed]).standard_normal(out[name].shape)
        drawn = base * np.exp(spread * noise) if base else spread * noise
        out[name] = jnp.asarray(drawn.astype(out[name].dtype))
    for name, factor in factors.items():
        out[name] = (out[name] * factor).astype(out[name].dtype)
    return out
```

```python
from contextlib import ExitStack

import concourse.bass as bass
from concourse import mybir

ALU = mybir.AluOpType
ACT = mybir.ActivationFunctionType
AX = mybir.AxisListType
F32 = mybir.dt.float32
I32 = mybir.dt.int32

P = 128
EPS = 1e-05

N = 12500
NT = -(-N // P)
NPAD = NT * P
NB = 7
HALF = 4
BATCHES = NT // NB
TAIL = N - (NT - 1) * P
assert BATCHES % 2 == 0 and BATCHES * NB == NT

E = 400000
T = 5
G = 5
GE = T * P
GROUPS = E // GE
CHUNKS = GROUPS // G
TILES = GROUPS * T
assert CHUNKS * G * GE == E

ED = 32
W = P - ED
BMAX = N - W
FN = N // CHUNKS
assert FN * CHUNKS == N
LAG = 2

D = 128
GATES = 3 * D
ROW = D + 4


def gnn_kernel(nc, x, src_cols, dst_cols, dst_rows, src_tiles, dst_tiles, ea_t, w1, b1, w2, b2, w_ih, b_ih, w_hh, b_hh, out):
    p_rows = nc.dram_tensor("p_rows", [NPAD, D], F32, kind="Internal").ap()
    q_rows = nc.dram_tensor("q_rows", [NPAD, D], F32, kind="Internal").ap()
    base_f_dram = nc.dram_tensor("base_f_dram", [CHUNKS, G], F32, kind="Internal").ap()
    base_i_dram = nc.dram_tensor("base_i_dram", [CHUNKS, G], I32, kind="Internal").ap()

    sum_rows = nc.dram_tensor("sum_rows", [NPAD, ROW], F32, kind="Internal").ap()

    with ExitStack() as ctx:
        def sb(name, shape, dt=F32):
            return ctx.enter_context(nc.sbuf_tensor(name, shape, dt))

        def sem(name):
            return ctx.enter_context(nc.semaphore(name))

        def sems(name, n):
            return [sem(f"{name}{i}") for i in range(n)]

        acc = sb("acc", [P, NPAD])
        xt = acc[:, :].rearrange("p (n f) -> p n f", f=D)
        hT = sb("hT", [P, NPAD])
        low = sb("low", [P, NPAD])
        deg = low[0:1, :]
        SW = NB * 2 * D
        stage = [low[:, k * SW:(k + 1) * SW].rearrange("p (n f) -> p n f", f=2 * D) for k in range(2)]
        at = 2 * SW
        dst_nat = low[0:CHUNKS, at:at + G * GE].bitcast(I32)
        at += G * GE
        base_bc = low[:, at:at + GROUPS]
        at += GROUPS
        w1ab = low[:, at:at + 2 * D]
        at += 2 * D
        w2_sb = low[:, at:at + D]
        at += D
        w2T = low[:, at:at + D]
        at += D
        wih_sb = low[:, at:at + GATES]
        at += GATES
        b1_bc = low[:, at:at + D]
        at += D
        xn = [low[:, at + k * NB * D:at + (k + 1) * NB * D] for k in range(2)]
        at += 2 * NB * D
        hT_batch = [low[:, at + k * NB * D:at + (k + 1) * NB * D] for k in range(2)]
        at += 2 * NB * D
        assert at <= NPAD

        dst_int = sb("dst_int", [P, GROUPS * T], I32)
        dst_rel = dst_int[:, :].bitcast(F32)
        rows = sb("rows", [P, G, T, D])
        onehot = sb("onehot", [P, G, T, W])
        lhs = sb("lhs", [P, G, GE])
        rhs = sb("rhs", [P, G, D])
        idx = sb("idx", [P, G, T], I32)
        base_i = sb("base_i", [1, GROUPS], I32)
        ident = sb("ident", [P, P])
        iota_w = sb("iota_w", [P, W])
        ones = sb("ones", [P, 1])
        w2ih = sb("w2ih", [P, GATES])
        whh_sb = sb("whh_sb", [P, GATES])
        b2_col = sb("b2_col", [P, 1])
        b2ih = sb("b2ih", [1, GATES])
        bih_col = sb("bih_col", [P, 3])
        bhh_col = sb("bhh_col", [P, 3])
        brz_col = sb("brz_col", [P, 2])
        eps_col = sb("eps_col", [P, 1])
        zero1 = sb("zero1", [1, 1])
        stats = sb("stats", [P, 2, NB, 6])
        mv = sb("mv", [P, 2, NB, 2])
        std = sb("std", [P, 2, NB])
        rstd = sb("rstd", [P, 2, NB])
        gmin = sb("gmin", [P, G])
        gmax = sb("gmax", [P, G])
        base_f = sb("base_f", [P, G])
        base_n = sb("base_n", [P, G], I32)
        viol = sb("viol", [P, 4])
        floor_c = sb("floor_c", [P, 1])
        flag_f = sb("flag_f", [1, 1])
        flag_i = sb("flag_i", [1, 1], I32)
        rz = sb("rz", [P, 2, FN])
        cand = sb("cand", [P, FN])
        upd = sb("upd", [P, FN])
        x_fin = sb("x_fin", [FN, D])
        out_fin = sb("out_fin", [FN, D])

        g_src, g_dst, g_out_idx = (idx[:, 0, k:k + 1] for k in range(3))
        g_p, g_q = rows[:, 0, 0, :], rows[:, 0, 1, :]
        g_sum, g_new = (rows[:, k, 0:2, :].rearrange("p t f -> p (t f)")[:, 0:ROW] for k in (1, 2))
        g_bc, g_eq, g_dup = (rows[:, 3, k, :] for k in range(3))
        g_earlier = rows[:, 4, 0, :]
        g_zero = rows[:, 4, 1:3, :].rearrange("p t f -> p (t f)")[:, 0:ROW]
        g_cols = sb("g_cols", [P, 4])
        g_dstf, g_count, g_isdup, g_outf = (g_cols[:, k:k + 1] for k in range(4))

        ps = ctx.enter_context(nc.psum_tensor("ps", [P, 4096], F32))
        onehotT_ps = ps[0:W, 0:GE]
        pre_ps = [ps[:, 1024 + k * 1024:1024 + k * 1024 + GE] for k in range(2)]
        seg_ps = ps[:, 3072:3072 + 2 * W]
        g_dst_ps = ps[:, 0:P]
        gate_ps = ps[:, 3584:3584 + 4 * FN].rearrange("p (g n) -> p g n", g=4)
        back_ps = ps[0:FN, 3584:3584 + D]
        gate_ps1 = ps[0:1, 3584:3584 + P]
        xT_ps = [ps[:, k * 1024:k * 1024 + NB * D] for k in range(2)]
        pq_ps = [ps[:, 2048:2048 + HALF * 2 * D].rearrange("p (n f) -> p n f", f=2 * D),
                 ps[:, 3072:3072 + (NB - HALF) * 2 * D].rearrange("p (n f) -> p n f", f=2 * D)]
        setup_ps = ps[:, 0:512]

        w1_in, weights_in, bias_in, dst_in, dstn_in, b1_in = (sem(n) for n in ("w1_in", "weights_in", "bias_in", "dst_in", "dstn_in", "b1_in"))
        ident_zeroed, consts_ready, ranges_ready, viol_ready, violT_ready, flag_ready = (sem(n) for n in (
            "ident_zeroed", "consts_ready", "ranges_ready", "viol_ready", "violT_ready", "flag_ready"))
        base_stored, base_bc_in, base_i_in, eps_set, dve_chain = (sem(n) for n in ("base_stored", "base_bc_in", "base_i_in", "eps_set", "dve_chain"))
        w2T_ready, w2T_copied, w2ih_ready, w2ih_copied = (sem(n) for n in ("w2T_ready", "w2T_copied", "w2ih_ready", "w2ih_copied"))
        pad_zeroed, x_tail_in = sem("pad_zeroed"), sem("x_tail_in")
        x_in = sems("x_in", 2)
        stats_done, aggr_done, std_ready, rstd_done = (sems(n, 2) for n in ("stats_done", "aggr_done", "std_ready", "rstd_done"))
        xn_ready, xT_ready, hT_ready, hT_kept = (sems(n, 2) for n in ("xn_ready", "xT_ready", "hT_ready", "hT_kept"))
        pq_ready = sems("pq_ready", 2)
        pq_copied = sems("pq_copied", 2)
        q_biased, pq_stored = (sems(n, 2) for n in ("q_biased", "pq_stored"))
        dst_rel_ready, acc_zeroed, deg_zeroed = sem("dst_rel_ready"), sem("acc_zeroed"), sem("deg_zeroed")
        idx_in, ea_in, q_in, rows_in = (sems(n, G) for n in ("idx_in", "ea_in", "q_in", "rows_in"))
        onehot_ready, onehotT_ready, lhs_ready, pre_ready = (sems(n, G) for n in ("onehot_ready", "onehotT_ready", "lhs_ready", "pre_ready"))
        summed, message_ready, seg_ready, acc_added = (sems(n, G) for n in ("summed", "message_ready", "seg_ready", "acc_added"))
        gates_ready, rz_ready, n_pre_ready, cand_ready, upd_ready, back_ready, out_ready, x_fin_in, stored = (sem(n) for n in (
            "gates_ready", "rz_ready", "n_pre_ready", "cand_ready", "upd_ready", "back_ready", "out_ready", "x_fin_in", "stored"))
        fin_chain = sem("fin_chain")
        g_zeroed, g_mask_set, g_scattered, g_chain = (sem(n) for n in ("g_zeroed", "g_mask_set", "g_scattered", "g_chain"))
        g_src_in, g_dst_in, g_ea_in = (sem(n) for n in ("g_src_in", "g_dst_in", "g_ea_in"))
        g_gathered = sems("g_gathered", 3)
        g_bc_ready, g_bcT_ready, g_pre_ready, g_summed, g_message_ready, g_seg_ready, g_new_ready = (sem(n) for n in (
            "g_bc_ready", "g_bcT_ready", "g_pre_ready", "g_summed", "g_message_ready", "g_seg_ready", "g_new_ready"))
        g_sums_in, g_sumsT_ready, g_sumsT_kept = (sem(n) for n in ("g_sums_in", "g_sumsT_ready", "g_sumsT_kept"))

        block = ctx.enter_context(nc.Block())

        def wait(eng, s, value):
            if not (isinstance(value, int) and value <= 0):
                eng.wait_ge(s, value)

        def before(c, s, back):
            c2, s2 = (c, s - back) if s >= back else (c - 1, s - back + G)
            return None if isinstance(c, int) and c2 < 0 else (c2, s2)

        def over_chunks(eng, body):
            for c in range(LAG + 1):
                body(c)
            with eng.Fori(LAG + 1, CHUNKS) as c:
                body(c)

        def over_fin(eng, body):
            body(0)
            with eng.Fori(1, CHUNKS) as n:
                body(n)

        def choose(eng, fast, general):
            eng.wait_ge(flag_ready, 1)
            misfit = eng.value_load(flag_i[0:1, 0:1], min_val=0, max_val=1)
            with eng.If(misfit == 0):
                fast()
            with eng.Else():
                general()

        @block.sync
        def _(sp):
            sp.dma_start(w1ab[:, 0:D], w1[0:D, :]).then_inc(w1_in, 16)
            sp.dma_start(w1ab[:, D:2 * D], w1[D:2 * D, :]).then_inc(w1_in, 16)

            def load_x(k, par):
                xv = x[0:(NT - 1) * P, :].rearrange("(n p) f -> p n f", p=P)
                sp.dma_start(xt[:, bass.ds(k * NB, NB), :], xv[:, bass.ds(k * NB, NB), :]).then_inc(x_in[par], 16)

            load_x(0, 0)
            load_x(1, 1)
            sp.wait_ge(pad_zeroed, 1)
            sp.dma_start(xt[0:TAIL, NT - 1, :], x[(NT - 1) * P:N, :]).then_inc(x_tail_in, 16)
            with sp.Fori(1, BATCHES // 2 - 1) as i:
                for par in range(2):
                    sp.wait_ge(x_in[par], i * 16)
                    load_x(i * 2 + par, par)
            k = BATCHES - 2
            sp.wait_ge(x_in[0], k // 2 * 16)
            load_x(k, 0)
            sp.wait_ge(x_in[1], k // 2 * 16)
            k = BATCHES - 1
            xv = x[0:(NT - 1) * P, :].rearrange("(n p) f -> p n f", p=P)
            sp.dma_start(xt[:, k * NB:NT - 1, :], xv[:, k * NB:NT - 1, :]).then_inc(x_in[1], 16)
            for s in range(G):
                sp.dma_start(rhs[W:P, s, :], w1[2 * D:2 * D + ED, :]).then_inc(weights_in, 16)
            sp.dma_start(w2_sb, w2).then_inc(weights_in, 16)
            sp.dma_start(wih_sb, w_ih).then_inc(weights_in, 16)
            sp.dma_start(whh_sb[:], w_hh).then_inc(weights_in, 16)
            for par in range(2):
                sp.wait_ge(pq_stored[par], BATCHES // 2 * 32)
            sp.wait_ge(base_i_in, 16)

            def load_group(c, s):
                wait(sp, rows_in[s], c * (16 * T))
                sp.dma_start(idx[:, s, :], src_cols[bass.ds(c * (G * P) + s * P, P), :]).then_inc(idx_in[s], 16)
                wait(sp, pre_ready[s], c)
                sp.dma_start(lhs[W:P, s, :], ea_t[:, bass.ds(c * (G * GE) + s * GE, GE)]).then_inc(ea_in[s], 16)
                b = sp.value_load(base_i[0:1, bass.ds(c * G + s, 1)], min_val=0, max_val=BMAX)
                sp.dma_start(rhs[0:W, s, :], q_rows[bass.ds(b, W), :]).then_inc(q_in[s], 16)

            def chunk(c):
                for s in range(G):
                    load_group(c, s)

            def general():
                with sp.Fori(0, TILES) as t:
                    sp.wait_ge(g_scattered, t * 16 + 16)
                    sp.dma_start(g_src, src_tiles[bass.ds(t, 1), :].rearrange("o p -> p o")).then_inc(g_src_in, 16)
                    sp.dma_start(g_dst, dst_tiles[bass.ds(t, 1), :].rearrange("o p -> p o")).then_inc(g_dst_in, 16)
                    sp.dma_start(lhs[W:P, 0, 0:P], ea_t[:, bass.ds(t * P, P)]).then_inc(g_ea_in, 16)
                sp.wait_ge(g_scattered, TILES * 16 + 16)

                def load_sums(j):
                    wait(sp, g_sumsT_ready, j)
                    sp.dma_start(g_sum, sum_rows[bass.ds(j * P, P), :]).then_inc(g_sums_in, 16)
                load_sums(0)
                with sp.Fori(1, NT) as j:
                    load_sums(j)
            choose(sp, lambda: over_chunks(sp, chunk), general)

        @block.gpsimd
        def _(pool):
            nc.gpsimd.memset(ident[:], 0.0).then_inc(ident_zeroed, 1)
            nc.gpsimd.memset(xt[:, NT - 1, :], 0.0).then_inc(pad_zeroed, 1)
            nc.gpsimd.memset(ones[:], 1.0)
            nc.gpsimd.memset(zero1[:], 0.0)
            nc.gpsimd.iota(iota_w[:], [[1, W]], base=0, channel_multiplier=0, allow_small_or_imprecise_dtypes=True)
            nc.gpsimd.iota(floor_c[:], [[1, 1]], base=-FN, channel_multiplier=FN, allow_small_or_imprecise_dtypes=True)
            pool.wait_ge(ident_zeroed, 1)
            nc.gpsimd.affine_select(out=ident[:], in_=ident[:], compare_op=ALU.not_equal, fill=1.0, base=0,
                                    pattern=[[-1, P]], channel_multiplier=1).then_inc(consts_ready, 1)
            pool.wait_ge(b1_in, 16)
            pv = p_rows.rearrange("(n p) f -> p n f", p=P)
            qv = q_rows.rearrange("(n p) f -> p n f", p=P)
            with pool.Fori(0, BATCHES // 2) as i:
                for par in range(2):
                    for half in range(2):
                        pool.wait_ge(pq_copied[half], i * 2 + par + 1)
                    qs = stage[par][:, :, D:2 * D]
                    nc.gpsimd.tensor_tensor(qs, qs, b1_bc.unsqueeze(1).to_broadcast([P, NB, D]), ALU.add).then_inc(q_biased[par], 1)
                    pool.wait_ge(b1_in, 16)
                    pool.wait_ge(q_biased[par], i + 1)
                    pool.dma_start(pv[:, bass.ds((i * 2 + par) * NB, NB), :], stage[par][:, :, 0:D]).then_inc(pq_stored[par], 16)
                    pool.dma_start(qv[:, bass.ds((i * 2 + par) * NB, NB), :], qs).then_inc(pq_stored[par], 16)
            for par in range(2):
                pool.wait_ge(pq_stored[par], BATCHES // 2 * 32)

            arrived_reg = pool.alloc_register("indices_arrived")

            def chunk(c):
                arrived = c * 16 + 16
                if not isinstance(c, int):
                    pool.reg_add(arrived_reg, c * 16, 16)
                    arrived = arrived_reg
                for s in range(G):
                    pool.wait_ge(pq_stored[1], BATCHES // 2 * 32)
                    pool.wait_ge(idx_in[s], arrived)
                    wait(pool, seg_ready[s], c)
                    for t in range(T):
                        pool.indirect_dma_start(
                            out=rows[:, s, t, :], out_offset=None, in_=p_rows[:, :],
                            in_offset=bass.IndirectOffsetOnAxis(ap=idx[:, s, t:t + 1], axis=0)).then_inc(rows_in[s], 16)

            def general():
                nc.gpsimd.memset(g_zero, 0.0).then_inc(g_zeroed, 1)
                nc.gpsimd.memset(g_earlier, 1.0).then_inc(g_zeroed, 1)
                pool.wait_ge(g_zeroed, 2)
                nc.gpsimd.affine_select(out=g_earlier, in_=g_earlier, compare_op=ALU.is_gt, fill=0.0, base=0,
                                        pattern=[[-1, P]], channel_multiplier=1).then_inc(g_mask_set, 1)
                pool.dma_start(sum_rows.rearrange("(n p) f -> p n f", p=P),
                               g_zero.unsqueeze(1).to_broadcast([P, NT, ROW])).then_inc(g_scattered, 16)
                arrived = pool.alloc_register("tile_arrived")
                with pool.Fori(0, TILES) as t:
                    pool.reg_add(arrived, t * 16, 16)
                    pool.wait_ge(pq_stored[1], BATCHES // 2 * 32)
                    pool.wait_ge(g_src_in, arrived)
                    pool.wait_ge(g_dst_in, arrived)
                    pool.wait_ge(g_scattered, arrived)
                    for gathered, (buffer, table, index) in zip(g_gathered, ((g_p, p_rows, g_src), (g_q, q_rows, g_dst), (g_sum, sum_rows, g_dst))):
                        pool.indirect_dma_start(out=buffer, out_offset=None, in_=table[:, :],
                                                in_offset=bass.IndirectOffsetOnAxis(ap=index, axis=0)).then_inc(gathered, 16)
                    pool.reg_add(arrived, t, 1)
                    pool.wait_ge(flag_ready, 1)
                    pool.wait_ge(g_new_ready, arrived)
                    pool.indirect_dma_start(out=sum_rows[:, :], out_offset=bass.IndirectOffsetOnAxis(ap=g_out_idx, axis=0),
                                            in_=g_new, in_offset=None, bounds_check=NPAD - 1,
                                            oob_is_err=False).then_inc(g_scattered, 16)
            choose(pool, lambda: over_chunks(pool, chunk), general)

        @block.scalar
        def _(act):
            act.dma_start(dst_nat, dst_rows).then_inc(dstn_in, 16)
            act.dma_start(dst_int[:], dst_cols).then_inc(dst_in, 16)
            act.dma_start(b1_bc, b1.unsqueeze(0).to_broadcast([P, D])).then_inc(b1_in, 16)
            act.dma_start(b2_col[:], b2.unsqueeze(1)).then_inc(bias_in, 16)
            act.dma_start(bih_col[:], b_ih).then_inc(bias_in, 16)
            act.dma_start(bhh_col[:], b_hh).then_inc(bias_in, 16)
            act.wait_ge(ranges_ready, 1)
            act.dma_start(base_f_dram, base_f[0:CHUNKS, :]).then_inc(base_stored, 16)
            act.dma_start(base_i_dram, base_n[0:CHUNKS, :]).then_inc(base_stored, 16)
            act.wait_ge(base_stored, 32)
            act.dma_start(base_i[:], base_i_dram.rearrange("(o c) g -> o (c g)", o=1)).then_inc(base_i_in, 16)
            act.dma_start(base_bc, base_f_dram.rearrange("(o c) g -> o (c g)", o=1).to_broadcast([P, GROUPS])).then_inc(base_bc_in, 16)

            act.wait_ge(eps_set, 1)

            def batches(i, first):
                for par in range(2):
                    act.wait_ge(aggr_done[par], i + 1)
                    nc.scalar.activation(std[:, par, :], mv[:, par, :, 1], ACT.Sqrt, bias=eps_col[:]).then_inc(std_ready[par], 1)
                for par in range(2):
                    act.wait_ge(xT_ready[par], i + 1)
                    if not first:
                        act.wait_ge(pq_ready[1], i * 2 + par - 1)
                    nc.scalar.activation(hT_batch[par], xT_ps[par], ACT.Relu).then_inc(hT_ready[par], 1)
                    nc.scalar.activation(hT[:, bass.ds((i * 2 + par) * (NB * D), NB * D)], xT_ps[par], ACT.Relu).then_inc(hT_kept[par], 1)
                    if not first:
                        act.wait_ge(pq_stored[par], i * 32)
                    act.wait_ge(pq_ready[0], i * 2 + par + 1)
                    nc.scalar.copy(stage[par][:, 0:HALF, :], pq_ps[0]).then_inc(pq_copied[0], 1)
                    act.wait_ge(pq_ready[1], i * 2 + par + 1)
                    nc.scalar.copy(stage[par][:, HALF:NB, :], pq_ps[1]).then_inc(pq_copied[1], 1)
            batches(0, True)
            with act.Fori(1, BATCHES // 2) as i:
                batches(i, False)

            act.wait_ge(w2T_ready, 1)
            nc.scalar.copy(w2T, setup_ps[:, 0:D]).then_inc(w2T_copied, 1)
            act.wait_ge(w2ih_ready, 1)
            nc.scalar.copy(w2ih[:], setup_ps[:, 0:GATES]).then_inc(w2ih_copied, 1)
            act.wait_ge(w2ih_ready, 2)
            nc.scalar.copy(b2ih[:], setup_ps[0:1, 0:GATES]).then_inc(w2ih_copied, 1)
            for par in range(2):
                act.wait_ge(pq_stored[par], BATCHES // 2 * 32)
            act.wait_ge(dst_rel_ready, 1)
            nc.scalar.copy(deg[0:1, 0:N], zero1[0:1, 0:1].to_broadcast([1, N])).then_inc(deg_zeroed, 1)

            def copy_onehot(c, s):
                act.wait_ge(onehotT_ready[s], c + 1)
                wait(act, pre_ready[s], c)
                nc.scalar.copy(lhs[0:W, s, :], onehotT_ps).then_inc(lhs_ready[s], 1)

            def relu_message(c, s):
                act.wait_ge(summed[s], c + 1)
                m = rows[:, s, :, :]
                nc.scalar.activation(m, m, ACT.Relu).then_inc(message_ready[s], 1)

            def load_x_fin(n):
                wait(act, out_ready, n)
                act.dma_start(x_fin[:], x[bass.ds(n * FN, FN), :]).then_inc(x_fin_in, 16)

            def gate_activations(n):
                act.wait_ge(gates_ready, n + 1)
                wait(act, upd_ready, n)
                for g in range(2):
                    last = nc.scalar.activation(rz[:, g, :], gate_ps[:, g, :], ACT.Sigmoid, bias=brz_col[:, g:g + 1])
                last.then_inc(rz_ready, 1)

            def candidate(n):
                act.wait_ge(n_pre_ready, n + 1)
                nc.scalar.activation(cand[:], cand[:], ACT.Tanh, bias=bih_col[:, 2:3]).then_inc(cand_ready, 1)

            def store(n):
                act.wait_ge(out_ready, n + 1)
                act.dma_start(out[bass.ds(n * FN, FN), :], out_fin[:]).then_inc(stored, 16)

            def chunk(c):
                live = not isinstance(c, int) or c >= LAG
                n = c - LAG
                if live:
                    load_x_fin(n)
                for s in range(G):
                    copy_onehot(c, s)
                    old = before(c, s, 2)
                    if old:
                        relu_message(*old)
                    if live and s == 3:
                        gate_activations(n)
                        candidate(n)
                    if live and s == 4:
                        store(n)

            def fin(n):
                load_x_fin(n)
                gate_activations(n)
                candidate(n)
                store(n)

            def fast():
                over_chunks(act, chunk)
                for back in (2, 1):
                    relu_message(CHUNKS - 1, G - back)
                for n in range(CHUNKS - LAG, CHUNKS):
                    fin(n)

            def general():
                with act.Fori(0, TILES) as t:
                    act.wait_ge(g_summed, t + 1)
                    nc.scalar.activation(g_p, g_p, ACT.Relu).then_inc(g_message_ready, 1)
                with act.Fori(0, NT) as j:
                    act.wait_ge(g_sumsT_ready, j + 1)
                    nc.scalar.copy(acc[:, bass.ds(j * P, P)], seg_ps[:, 0:P])
                    nc.scalar.copy(deg[0:1, bass.ds(j * P, P)], gate_ps1[0:1, 0:P]).then_inc(g_sumsT_kept, 1)
                over_fin(act, fin)
            choose(act, fast, general)
            act.wait_ge(stored, CHUNKS * 16)

        @block.vector
        def _(dve):
            chain = [0]

            def link(ins):
                chain[0] += 1
                ins.then_inc(dve_chain, 1)
                dve.wait_ge(dve_chain, chain[0])

            nc.vector.memset(eps_col[:], EPS).then_inc(eps_set, 1)
            dve.wait_ge(dstn_in, 16)
            dn = dst_nat.rearrange("c (g e) -> c g e", g=G)
            nc.vector.tensor_reduce(gmin[0:CHUNKS, :], dn, AX.X, ALU.min)
            link(nc.vector.tensor_reduce(gmax[0:CHUNKS, :], dn, AX.X, ALU.max))
            link(nc.vector.tensor_scalar(base_f[0:CHUNKS, :], gmin[0:CHUNKS, :], float(BMAX), None, ALU.min))
            nc.vector.tensor_copy(base_n[0:CHUNKS, :], base_f[0:CHUNKS, :]).then_inc(ranges_ready, 1)
            link(nc.vector.tensor_tensor(gmax[0:CHUNKS, :], gmax[0:CHUNKS, :], base_f[0:CHUNKS, :], ALU.subtract))
            nc.vector.tensor_reduce(viol[0:CHUNKS, 0:1], gmax[0:CHUNKS, :], AX.X, ALU.max)
            link(nc.vector.tensor_reduce(viol[0:CHUNKS, 1:2], gmin[0:CHUNKS, :], AX.X, ALU.min))
            nc.vector.tensor_scalar(viol[0:CHUNKS, 0:1], viol[0:CHUNKS, 0:1], float(W - 1), None, ALU.subtract)
            dve.wait_ge(consts_ready, 1)
            link(nc.vector.tensor_tensor(viol[0:CHUNKS, 1:2], floor_c[0:CHUNKS, :], viol[0:CHUNKS, 1:2], ALU.subtract))
            nc.vector.tensor_tensor(viol[0:CHUNKS, 2:3], viol[0:CHUNKS, 0:1], viol[0:CHUNKS, 1:2], ALU.max).then_inc(viol_ready, 1)
            dve.wait_ge(violT_ready, 1)
            link(nc.vector.tensor_reduce(flag_f[:], setup_ps[0:1, 0:CHUNKS], AX.X, ALU.max))
            nc.vector.tensor_scalar(flag_i[:], flag_f[:], 0.0, None, ALU.is_gt).then_inc(flag_ready, 1)

            dve.wait_ge(x_tail_in, 16)

            turn_reg = dve.alloc_register("turn")

            def batches(i, first):
                turn = 1
                if not first:
                    dve.reg_add(turn_reg, i, 1)
                    turn = turn_reg
                for par in range(2):
                    k = i * 2 + par
                    dve.wait_ge(x_in[par], i * 16 + 16)
                    for t in range(NB):
                        last = nc.vector.bn_stats(stats[:, par, t, :], acc[:, bass.ds(k * (NB * D) + t * D, D)])
                    last.then_inc(stats_done[par], 1)
                    dve.wait_ge(x_tail_in, 16)
                    dve.wait_ge(stats_done[par], turn)
                    for t in range(NB):
                        last = nc.vector.bn_aggr(mv[:, par, t, :], stats[:, par, t, :])
                    last.then_inc(aggr_done[par], 1)
                for par in range(2):
                    k = i * 2 + par
                    dve.wait_ge(std_ready[par], i + 1)
                    nc.vector.reciprocal(rstd[:, par, :], std[:, par, :]).then_inc(rstd_done[par], 1)
                    dve.wait_ge(rstd_done[par], i + 1)
                    if not first:
                        dve.wait_ge(xT_ready[par], i)
                    for t in range(NB):
                        xr = acc[:, bass.ds(k * (NB * D) + t * D, D)]
                        last = nc.vector.tensor_scalar(xn[par][:, t * D:(t + 1) * D], xr, mv[:, par, t, 0:1], rstd[:, par, t:t + 1],
                                                       ALU.subtract, ALU.mult)
                    last.then_inc(xn_ready[par], 1)
            batches(0, True)
            with dve.Fori(1, BATCHES // 2) as i:
                batches(i, False)

            dve.wait_ge(bias_in, 48)
            nc.vector.tensor_tensor(brz_col[:], bih_col[:, 0:2], bhh_col[:, 0:2], ALU.add)
            dve.wait_ge(base_bc_in, 16)
            dve.wait_ge(dst_in, 16)
            dr = dst_rel.rearrange("p (g t) -> p g t", t=T)
            nc.vector.tensor_tensor(dr, dst_int[:, :].rearrange("p (g t) -> p g t", t=T),
                                    base_bc.unsqueeze(2).to_broadcast([P, GROUPS, T]), ALU.subtract).then_inc(dst_rel_ready, 1)
            dve.wait_ge(dst_rel_ready, 1)

            def build_onehot(c, s):
                wait(dve, seg_ready[s], c)
                d = dst_rel[:, bass.ds(c * (G * T) + s * T, T)]
                nc.vector.tensor_tensor(onehot[:, s, :, :], iota_w[:, :].unsqueeze(1).to_broadcast([P, T, W]),
                                        d.unsqueeze(2).to_broadcast([P, T, W]), ALU.is_equal).then_inc(onehot_ready[s], 1)

            def add_pre(c, s):
                dve.wait_ge(pre_ready[s], c + 1)
                dve.wait_ge(rows_in[s], c * (16 * T) + 16 * T)
                r = rows[:, s, :, :].rearrange("p t f -> p (t f)")
                nc.vector.tensor_tensor(r, r, pre_ps[s % 2], ALU.add).then_inc(summed[s], 1)

            def add_segments(c, s, prev):
                dve.wait_ge(seg_ready[s], c + 1)
                if prev:
                    dve.wait_ge(acc_added[prev[1]], prev[0] * 2 + 2)
                b = dve.value_load(base_i[0:1, bass.ds(c * G + s, 1)], min_val=0, max_val=BMAX)
                sg = seg_ps
                nc.vector.tensor_tensor(acc[:, bass.ds(b, W)], acc[:, bass.ds(b, W)], sg[:, 0:W], ALU.add).then_inc(acc_added[s], 1)
                nc.vector.tensor_tensor(deg[0:1, bass.ds(b, W)], deg[0:1, bass.ds(b, W)], sg[0:1, W:2 * W],
                                        ALU.add).then_inc(acc_added[s], 1)

            def candidate_pre(n):
                dve.wait_ge(rz_ready, n + 1)
                nc.vector.scalar_tensor_tensor(out=upd[:], in0=gate_ps[:, 3, :], scalar=bhh_col[:, 2:3], in1=rz[:, 0, :],
                                               op0=ALU.add, op1=ALU.mult).then_inc(fin_chain, 1)
                dve.wait_ge(fin_chain, n * 3 + 1)
                nc.vector.tensor_tensor(cand[:], upd[:], gate_ps[:, 2, :], ALU.add).then_inc(n_pre_ready, 1)

            def update(n):
                dve.wait_ge(cand_ready, n + 1)
                h = hT[:, bass.ds(n * FN, FN)]
                nc.vector.tensor_tensor(upd[:], h, cand[:], ALU.subtract).then_inc(fin_chain, 1)
                dve.wait_ge(fin_chain, n * 3 + 2)
                nc.vector.tensor_tensor(upd[:], upd[:], rz[:, 1, :], ALU.mult).then_inc(fin_chain, 1)
                dve.wait_ge(fin_chain, n * 3 + 3)
                nc.vector.tensor_tensor(upd[:], upd[:], cand[:], ALU.add).then_inc(upd_ready, 1)

            def residual(n):
                dve.wait_ge(back_ready, n + 1)
                dve.wait_ge(x_fin_in, n * 16 + 16)
                wait(dve, stored, n * 16)
                nc.vector.tensor_tensor(out_fin[:], x_fin[:], back_ps, ALU.add).then_inc(out_ready, 1)

            def chunk(c):
                live = not isinstance(c, int) or c >= LAG
                n = c - LAG
                for s in range(G):
                    build_onehot(c, s)
                    old = before(c, s, 2)
                    if old:
                        add_pre(*old)
                    old = before(c, s, 3)
                    if old:
                        if isinstance(c, int) and c == 0 and s == 3:
                            dve.wait_ge(deg_zeroed, 1)
                        add_segments(*old, before(c, s, 4))
                    if isinstance(c, int) and c == 0 and s == 0:
                        nc.vector.memset(acc[:, 0:N], 0.0).then_inc(acc_zeroed, 1)
                        dve.wait_ge(acc_zeroed, 1)
                    if live and s == 3:
                        candidate_pre(n)
                    if live and s == 4:
                        update(n)
                        residual(n)

            def fin(n):
                candidate_pre(n)
                update(n)
                residual(n)

            def fast():
                over_chunks(dve, chunk)
                c = CHUNKS - 1
                add_pre(c, G - 2)
                add_segments(c, G - 3, (c, G - 4))
                add_pre(c, G - 1)
                add_segments(c, G - 2, (c, G - 3))
                add_segments(c, G - 1, (c, G - 2))
                for n in range(CHUNKS - LAG, CHUNKS):
                    fin(n)

            def general():
                dve.wait_ge(g_mask_set, 1)
                nc.vector.memset(g_new, 0.0)
                with dve.Fori(0, TILES) as t:
                    step = [0]
                    steps = 8

                    def then(ins):
                        step[0] += 1
                        ins.then_inc(g_chain, 1)
                        dve.wait_ge(g_chain, t * steps + step[0])

                    dve.wait_ge(g_dst_in, t * 16 + 16)
                    then(nc.vector.tensor_copy(g_dstf, g_dst))
                    nc.vector.tensor_copy(g_bc, g_dstf.to_broadcast([P, P])).then_inc(g_bc_ready, 1)
                    dve.wait_ge(g_bcT_ready, t + 1)
                    then(nc.vector.tensor_scalar(g_eq, g_dst_ps, g_dstf, None, ALU.is_equal))
                    then(nc.vector.tensor_reduce(g_count, g_eq, AX.X, ALU.add))
                    then(nc.vector.tensor_tensor(g_dup, g_eq, g_earlier, ALU.mult))
                    then(nc.vector.tensor_reduce(g_isdup, g_dup, AX.X, ALU.max))
                    then(nc.vector.scalar_tensor_tensor(out=g_outf, in0=g_isdup, scalar=float(2 * NPAD), in1=g_dstf,
                                                        op0=ALU.mult, op1=ALU.add))
                    then(nc.vector.tensor_copy(g_out_idx, g_outf))
                    dve.wait_ge(g_pre_ready, t + 1)
                    for gathered in g_gathered:
                        dve.wait_ge(gathered, t * 16 + 16)
                    then(nc.vector.tensor_tensor(g_p, g_p, pre_ps[0][:, 0:D], ALU.add))
                    assert step[0] == steps
                    nc.vector.tensor_tensor(g_p, g_p, g_q, ALU.add).then_inc(g_summed, 1)
                    nc.vector.tensor_tensor(g_new[:, D:D + 1], g_sum[:, D:D + 1], g_count, ALU.add)
                    dve.wait_ge(g_seg_ready, t + 1)
                    nc.vector.tensor_tensor(g_new[:, 0:D], g_sum[:, 0:D], seg_ps[:, 0:D], ALU.add).then_inc(g_new_ready, 1)
                over_fin(dve, fin)

            for par in range(2):
                dve.wait_ge(xT_ready[par], BATCHES // 2)
            choose(dve, fast, general)

        @block.tensor
        def _(pe):
            pe.wait_ge(consts_ready, 1)
            pe.wait_ge(viol_ready, 1)
            nc.tensor.transpose(setup_ps[0:1, 0:CHUNKS], viol[0:CHUNKS, 2:3], ident[0:CHUNKS, 0:CHUNKS]).then_inc(violT_ready, 1)
            pe.wait_ge(flag_ready, 1)
            pe.wait_ge(w1_in, 32)

            def batches(i, first):
                for par in range(2):
                    pe.wait_ge(xn_ready[par], i + 1)
                    if not first:
                        pe.wait_ge(hT_kept[par], i)
                    for t in range(NB):
                        last = nc.tensor.transpose(xT_ps[par][:, t * D:(t + 1) * D], xn[par][:, t * D:(t + 1) * D], ident[:])
                    last.then_inc(xT_ready[par], 1)
                for par in range(2):
                    k = i * 2 + par
                    pe.wait_ge(hT_ready[par], i + 1)
                    for t in range(NB):
                        half, u = divmod(t, HALF)
                        if u == 0:
                            wait(pe, pq_copied[half], k)
                        last = nc.tensor.matmul(pq_ps[half][:, u, :], hT_batch[par][:, t * D:(t + 1) * D], w1ab,
                                                start=True, stop=True)
                        if t in (HALF - 1, NB - 1):
                            last.then_inc(pq_ready[half], 1)
            batches(0, True)
            with pe.Fori(1, BATCHES // 2) as i:
                batches(i, False)

            for half in range(2):
                pe.wait_ge(pq_copied[half], BATCHES)
            pe.wait_ge(weights_in, 16 * (G + 3))
            nc.tensor.transpose(setup_ps[:, 0:D], w2_sb, ident[:]).then_inc(w2T_ready, 1)
            pe.wait_ge(w2T_copied, 1)
            nc.tensor.matmul(setup_ps[:, 0:GATES], w2T, wih_sb, start=True, stop=True).then_inc(w2ih_ready, 1)
            pe.wait_ge(w2ih_copied, 1)
            pe.wait_ge(bias_in, 48)
            nc.tensor.matmul(setup_ps[0:1, 0:GATES], b2_col[:], wih_sb, start=True, stop=True).then_inc(w2ih_ready, 1)
            pe.wait_ge(w2ih_copied, 2)

            def transpose_onehot(c, s):
                pe.wait_ge(onehot_ready[s], c + 1)
                old = before(c, s, 1)
                if old:
                    pe.wait_ge(lhs_ready[old[1]], old[0] + 1)
                for t in range(T):
                    last = nc.tensor.transpose(onehotT_ps[:, t * P:(t + 1) * P], onehot[:, s, t, :], ident[:])
                last.then_inc(onehotT_ready[s], 1)

            def pre_activation(c, s):
                old = before(c, s, {0: 1, 1: 3}.get(s, 2))
                if old:
                    pe.wait_ge(summed[old[1]], old[0] + 1)
                pe.wait_ge(lhs_ready[s], c + 1)
                pe.wait_ge(ea_in[s], c * 16 + 16)
                pe.wait_ge(q_in[s], c * 16 + 16)
                for t in range(T):
                    last = nc.tensor.matmul(pre_ps[s % 2][:, t * D:(t + 1) * D], lhs[:, s, t * P:(t + 1) * P],
                                            rhs[:, s, :], start=True, stop=True)
                last.then_inc(pre_ready[s], 1)

            def segment_sums(c, s):
                pe.wait_ge(message_ready[s], c + 1)
                old = before(c, s, 1)
                if old:
                    pe.wait_ge(acc_added[old[1]], old[0] * 2 + 2)
                sg = seg_ps
                for t in range(T):
                    nc.tensor.matmul(sg[:, 0:W], rows[:, s, t, :], onehot[:, s, t, :], start=(t == 0), stop=(t == T - 1))
                for t in range(T):
                    last = nc.tensor.matmul(sg[0:1, W:2 * W], ones[:], onehot[:, s, t, :], start=(t == 0), stop=(t == T - 1))
                last.then_inc(seg_ready[s], 1)

            def gates(n):
                if not (isinstance(n, int) and n == 0):
                    wait(pe, out_ready, n)
                a, d, h = (v[:, bass.ds(n * FN, FN)] for v in (acc, deg, hT))
                for g in range(3):
                    cols = slice(g * D, (g + 1) * D)
                    nc.tensor.matmul(gate_ps[:, g, :], w2ih[:, cols], a, start=True, stop=False)
                    last = nc.tensor.matmul(gate_ps[:, g, :], b2ih[0:1, cols], d, start=False, stop=(g == 2))
                    if g < 2:
                        nc.tensor.matmul(gate_ps[:, g, :], whh_sb[:, cols], h, start=False, stop=True)
                nc.tensor.matmul(gate_ps[:, 3, :], whh_sb[:, 2 * D:3 * D], h, start=True, stop=True).then_inc(gates_ready, 1)

            def back(n):
                pe.wait_ge(upd_ready, n + 1)
                nc.tensor.transpose(back_ps, upd[:], ident[:]).then_inc(back_ready, 1)

            def chunk(c):
                live = not isinstance(c, int) or c >= LAG
                n = c - LAG
                for s in range(G):
                    transpose_onehot(c, s)
                    old = before(c, s, 1)
                    if old:
                        pre_activation(*old)
                    old = before(c, s, 2)
                    if old:
                        segment_sums(*old)
                    if live and s == 2:
                        pe.wait_ge(acc_added[G - 1], c * 2)
                        gates(n)
                    if live and s == 4:
                        back(n)

            def fin(n):
                gates(n)
                back(n)

            def fast():
                over_chunks(pe, chunk)
                c = CHUNKS - 1
                pre_activation(c, G - 1)
                segment_sums(c, G - 2)
                segment_sums(c, G - 1)
                pe.wait_ge(acc_added[G - 1], CHUNKS * 2)
                for n in range(CHUNKS - LAG, CHUNKS):
                    fin(n)

            def general():
                with pe.Fori(0, TILES) as t:
                    pe.wait_ge(g_bc_ready, t + 1)
                    nc.tensor.transpose(g_dst_ps, g_bc, ident[:]).then_inc(g_bcT_ready, 1)
                    pe.wait_ge(g_ea_in, t * 16 + 16)
                    nc.tensor.matmul(pre_ps[0][:, 0:D], lhs[W:P, 0, 0:P], rhs[W:P, 0, :], start=True,
                                     stop=True).then_inc(g_pre_ready, 1)
                    pe.wait_ge(g_message_ready, t + 1)
                    nc.tensor.matmul(seg_ps[:, 0:D], g_eq, g_p, start=True, stop=True).then_inc(g_seg_ready, 1)

                def transpose_sums(j):
                    pe.wait_ge(g_sums_in, j * 16 + 16)
                    wait(pe, g_sumsT_kept, j)
                    nc.tensor.transpose(seg_ps[:, 0:P], g_sum[:, 0:D], ident[:])
                    nc.tensor.transpose(gate_ps1, g_sum[:, D:D + 1], ident[:]).then_inc(g_sumsT_ready, 1)
                transpose_sums(0)
                with pe.Fori(1, NT) as j:
                    transpose_sums(j)
                pe.wait_ge(g_sumsT_kept, NT)
                over_fin(pe, fin)
            choose(pe, fast, general)


_OUTS = [((N, D), "float32")]


def kernel(**inputs):
    import numpy as _np
    import concourse.bacc as _bacc
    from concourse import mybir as _mybir
    from concourse.bass_utils import run_bass_kernel_spmd as _run

    src = _np.asarray(inputs["src"])
    dst = _np.asarray(inputs["dst"])
    w = {k: _np.ascontiguousarray(inputs["L0_gnn_" + k]) for k in ("w1", "b1", "w2", "b2", "w_ih", "b_ih", "w_hh", "b_hh")}
    for k in ("b_ih", "b_hh"):
        w[k] = _np.ascontiguousarray(w[k].reshape(3, D).T)
    laid = {
        "x": _np.ascontiguousarray(inputs["x"]),
        "src_cols": _np.ascontiguousarray(src.reshape(GROUPS, T, P).transpose(0, 2, 1).reshape(GROUPS * P, T)),
        "dst_cols": _np.ascontiguousarray(dst.reshape(GROUPS * T, P).T),
        "dst_rows": _np.ascontiguousarray(dst.reshape(CHUNKS, G * GE)),
        "src_tiles": _np.ascontiguousarray(src.reshape(TILES, P)),
        "dst_tiles": _np.ascontiguousarray(dst.reshape(TILES, P)),
        "ea_t": _np.ascontiguousarray(_np.asarray(inputs["edge_attr_32"]).T),
        **w,
    }
    nc = _bacc.Bacc("TRN2", target_bir_lowering=False, num_devices=1)
    arrays, args = {}, []
    for name, a in laid.items():
        arrays[f"in_{name}_dram"] = a
        args.append(nc.dram_tensor(f"in_{name}_dram", a.shape, _mybir.dt.from_np(a.dtype), kind="ExternalInput").ap())
    for i, (shape, dtype) in enumerate(_OUTS):
        dt = _mybir.dt.from_np(_np.dtype(dtype))
        args.append(nc.dram_tensor(f"out_{i}_dram", shape, dt, kind="ExternalOutput").ap())
    gnn_kernel(nc, *args)
    r = _run(nc, [arrays], core_ids=[0])
    return r.results[0]["out_0_dram"]
```

```python
from contextlib import ExitStack

import concourse.bass as bass
from concourse import mybir

ALU = mybir.AluOpType
ACT = mybir.ActivationFunctionType
AX = mybir.AxisListType
F32 = mybir.dt.float32
I32 = mybir.dt.int32

P = 128
EPS = 1e-05

N = 12500
NT = -(-N // P)
NPAD = NT * P
NB = 7
BATCHES = NT // NB
TAIL = N - (NT - 1) * P
assert BATCHES % 2 == 0 and BATCHES * NB == NT

E = 400000
T = 5
G = 5
GE = T * P
GROUPS = E // GE
CHUNKS = GROUPS // G
TILES = GROUPS * T
assert CHUNKS * G * GE == E

ED = 32
W = P - ED
BMAX = N - W
FN = N // CHUNKS
assert FN * CHUNKS == N
LAG = 2

D = 128
GATES = 3 * D
ROW = D + 4


def gnn_kernel(nc, x, src_cols, dst_cols, dst_rows, src_tiles, dst_tiles, ea_t, w1, b1, w2, b2, w_ih, b_ih, w_hh, b_hh, out):
    p_rows = nc.dram_tensor("p_rows", [NPAD, D], F32, kind="Internal").ap()
    base_f_dram = nc.dram_tensor("base_f_dram", [CHUNKS, G], F32, kind="Internal").ap()
    base_i_dram = nc.dram_tensor("base_i_dram", [CHUNKS, G], I32, kind="Internal").ap()

    q_rows = nc.dram_tensor("q_rows", [NPAD, D], F32, kind="Internal").ap()
    sum_rows = nc.dram_tensor("sum_rows", [NPAD, ROW], F32, kind="Internal").ap()

    with ExitStack() as ctx:
        def sb(name, shape, dt=F32):
            return ctx.enter_context(nc.sbuf_tensor(name, shape, dt))

        def sem(name):
            return ctx.enter_context(nc.semaphore(name))

        def sems(name, n):
            return [sem(f"{name}{i}") for i in range(n)]

        acc = sb("acc", [P, NPAD])
        xt = acc[:, :].rearrange("p (n f) -> p n f", f=D)
        hT = sb("hT", [P, NPAD])
        low = sb("low", [P, NPAD])
        deg = low[0:1, :]
        SW = NB * D
        stage = [low[:, k * SW:(k + 1) * SW].rearrange("p (n f) -> p n f", f=D) for k in range(2)]
        at = 2 * SW
        dst_nat = low[0:CHUNKS, at:at + G * GE].bitcast(I32)
        at += G * GE
        base_bc = low[:, at:at + GROUPS]
        at += GROUPS
        w1_src = low[:, at:at + D]
        at += D
        w2_sb = low[:, at:at + D]
        at += D
        w2T = low[:, at:at + D]
        at += D
        wih_sb = low[:, at:at + GATES]
        at += GATES
        b1_bc = low[:, at:at + D]
        at += D
        xn = [low[:, at + k * NB * D:at + (k + 1) * NB * D] for k in range(2)]
        at += 2 * NB * D
        hT_batch = [low[:, at + k * NB * D:at + (k + 1) * NB * D] for k in range(2)]
        at += 2 * NB * D
        base_i = low[ED:ED + 1, at:at + GROUPS].bitcast(I32)
        at += GROUPS
        assert at <= NPAD

        dst_int = sb("dst_int", [P, GROUPS * T], I32)
        dst_rel = dst_int[:, :].bitcast(F32)
        rows = sb("rows", [P, G, T, D])
        onehot = sb("onehot", [P, G, T, W])
        lhs = sb("lhs", [P, G, GE])
        rhs = sb("rhs", [P, G, D])
        h_win = sb("h_win", [P, W])
        w1_dst = sb("w1_dst", [P, D])
        idx = sb("idx", [P, G, T], I32)
        count = sb("count", [W, G])
        ident = sb("ident", [P, P])
        iota_w = sb("iota_w", [P, W])
        w2ih = sb("w2ih", [P, GATES])
        whh_sb = sb("whh_sb", [P, GATES])
        b2_col = sb("b2_col", [P, 1])
        b2ih = sb("b2ih", [1, GATES])
        bih_col = sb("bih_col", [P, 3])
        bhh_col = sb("bhh_col", [P, 3])
        brz_col = sb("brz_col", [P, 2])
        eps_col = sb("eps_col", [P, 1])
        zero1 = sb("zero1", [1, 1])
        stats = sb("stats", [P, 2, NB, 6])
        mv = sb("mv", [P, 2, NB, 2])
        std = sb("std", [P, 2, NB])
        rstd = sb("rstd", [P, 2, NB])
        gmin = sb("gmin", [P, G])
        gmax = sb("gmax", [P, G])
        base_f = sb("base_f", [P, G])
        base_n = sb("base_n", [P, G], I32)
        viol = sb("viol", [P, 4])
        floor_c = sb("floor_c", [P, 1])
        flag_f = sb("flag_f", [1, 1])
        flag_i = sb("flag_i", [1, 1], I32)
        rz = sb("rz", [P, 2, FN])
        cand = sb("cand", [P, FN])
        upd = sb("upd", [P, FN])
        x_fin = sb("x_fin", [FN, D])
        out_fin = sb("out_fin", [FN, D])

        g_src, g_dst, g_out_idx = (idx[:, 0, k:k + 1] for k in range(3))
        g_p, g_q = rows[:, 0, 0, :], rows[:, 0, 1, :]
        g_sum, g_new = (rows[:, k, 0:2, :].rearrange("p t f -> p (t f)")[:, 0:ROW] for k in (1, 2))
        g_bc, g_eq, g_dup = (rows[:, 3, k, :] for k in range(3))
        g_earlier = rows[:, 4, 0, :]
        g_zero = rows[:, 4, 1:3, :].rearrange("p t f -> p (t f)")[:, 0:ROW]
        g_cols = sb("g_cols", [P, 4])
        g_dstf, g_count, g_isdup, g_outf = (g_cols[:, k:k + 1] for k in range(4))

        ps = ctx.enter_context(nc.psum_tensor("ps", [P, 4096], F32))
        onehotT_ps = ps[0:W, 0:GE]
        pre_ps = [ps[:, 1024 + k * 1024:1024 + k * 1024 + GE] for k in range(2)]
        seg_ps = ps[:, 3072:3072 + 2 * W]
        g_dst_ps = ps[:, 0:P]
        gate_ps = ps[:, 3584:3584 + 4 * FN].rearrange("p (g n) -> p g n", g=4)
        back_ps = ps[0:FN, 3584:3584 + D]
        gate_ps1 = ps[0:1, 3584:3584 + P]
        q_ps = ps[0:W, GE:GE + D]
        xT_ps = [ps[:, k * 1024:k * 1024 + NB * D] for k in range(2)]
        p_ps = [ps[:, 2048 + k * 1024:2048 + k * 1024 + NB * D] for k in range(2)]
        setup_ps = ps[:, 0:512]

        w1_in, weights_in, bias_in, dst_in, dstn_in, b1_in = (sem(n) for n in ("w1_in", "weights_in", "bias_in", "dst_in", "dstn_in", "b1_in"))
        ident_zeroed, consts_ready, ranges_ready, viol_ready, violT_ready, flag_ready = (sem(n) for n in (
            "ident_zeroed", "consts_ready", "ranges_ready", "viol_ready", "violT_ready", "flag_ready"))
        base_stored, base_bc_in, base_i_in, eps_set, dve_chain = (sem(n) for n in ("base_stored", "base_bc_in", "base_i_in", "eps_set", "dve_chain"))
        w2T_ready, w2T_copied, w2ih_ready, w2ih_copied = (sem(n) for n in ("w2T_ready", "w2T_copied", "w2ih_ready", "w2ih_copied"))
        pad_zeroed, x_tail_in = sem("pad_zeroed"), sem("x_tail_in")
        x_in = sems("x_in", 2)
        stats_done, aggr_done, std_ready, rstd_done = (sems(n, 2) for n in ("stats_done", "aggr_done", "std_ready", "rstd_done"))
        xn_ready, xT_ready, hT_ready, hT_kept = (sems(n, 2) for n in ("xn_ready", "xT_ready", "hT_ready", "hT_kept"))
        p_ready, p_copied, p_biased, p_stored = (sems(n, 2) for n in ("p_ready", "p_copied", "p_biased", "p_stored"))
        dst_rel_ready, acc_zeroed, deg_zeroed = sem("dst_rel_ready"), sem("acc_zeroed"), sem("deg_zeroed")
        idx_in, ea_in, rows_in, h_win_ready = (sems(n, G) for n in ("idx_in", "ea_in", "rows_in", "h_win_ready"))
        onehot_ready, onehotT_ready, lhs_ready, pre_ready = (sems(n, G) for n in ("onehot_ready", "onehotT_ready", "lhs_ready", "pre_ready"))
        summed, message_ready, seg_ready, acc_added = (sems(n, G) for n in ("summed", "message_ready", "seg_ready", "acc_added"))
        gates_ready, rz_ready, n_pre_ready, cand_ready, upd_ready, back_ready, out_ready, x_fin_in, stored = (sem(n) for n in (
            "gates_ready", "rz_ready", "n_pre_ready", "cand_ready", "upd_ready", "back_ready", "out_ready", "x_fin_in", "stored"))
        fin_chain = sem("fin_chain")
        g_zeroed, g_mask_set, g_scattered, g_chain = (sem(n) for n in ("g_zeroed", "g_mask_set", "g_scattered", "g_chain"))
        g_h_ready, g_q_ready, g_q_copied, g_q_stored = (sem(n) for n in ("g_h_ready", "g_q_ready", "g_q_copied", "g_q_stored"))
        g_src_in, g_dst_in, g_ea_in = (sem(n) for n in ("g_src_in", "g_dst_in", "g_ea_in"))
        g_gathered = sems("g_gathered", 3)
        g_bc_ready, g_bcT_ready, g_pre_ready, g_summed, g_message_ready, g_seg_ready, g_new_ready = (sem(n) for n in (
            "g_bc_ready", "g_bcT_ready", "g_pre_ready", "g_summed", "g_message_ready", "g_seg_ready", "g_new_ready"))
        g_sums_in, g_sumsT_ready, g_sumsT_kept = (sem(n) for n in ("g_sums_in", "g_sumsT_ready", "g_sumsT_kept"))

        block = ctx.enter_context(nc.Block())

        def wait(eng, s, value):
            if not (isinstance(value, int) and value <= 0):
                eng.wait_ge(s, value)

        def before(c, s, back):
            c2, s2 = (c, s - back) if s >= back else (c - 1, s - back + G)
            return None if isinstance(c, int) and c2 < 0 else (c2, s2)

        def over_chunks(eng, body):
            for c in range(LAG + 2):
                body(c)
            with eng.Fori(LAG + 2, CHUNKS) as c:
                body(c)

        def finishing(c):
            known = isinstance(c, int)
            return (c - LAG if not known or c >= LAG else None, c - LAG - 1 if not known or c > LAG else None)

        def over_fin(eng, body):
            body(0)
            with eng.Fori(1, CHUNKS) as n:
                body(n)

        def choose(eng, fast, general):
            eng.wait_ge(flag_ready, 1)
            misfit = eng.value_load(flag_i[0:1, 0:1], min_val=0, max_val=1)
            with eng.If(misfit == 0):
                fast()
            with eng.Else():
                general()

        @block.sync
        def _(sp):
            def load_x(k, par):
                xv = x[0:(NT - 1) * P, :].rearrange("(n p) f -> p n f", p=P)
                sp.dma_start(xt[:, bass.ds(k * NB, NB), :], xv[:, bass.ds(k * NB, NB), :]).then_inc(x_in[par], 16)

            load_x(0, 0)
            load_x(1, 1)
            sp.wait_ge(pad_zeroed, 1)
            sp.dma_start(xt[0:TAIL, NT - 1, :], x[(NT - 1) * P:N, :]).then_inc(x_tail_in, 16)
            sp.dma_start(w1_src, w1[0:D, :]).then_inc(w1_in, 16)
            with sp.Fori(1, BATCHES // 2 - 1) as i:
                for par in range(2):
                    sp.wait_ge(x_in[par], i * 16)
                    load_x(i * 2 + par, par)
            k = BATCHES - 2
            sp.wait_ge(x_in[0], k // 2 * 16)
            load_x(k, 0)
            sp.wait_ge(x_in[1], k // 2 * 16)
            k = BATCHES - 1
            xv = x[0:(NT - 1) * P, :].rearrange("(n p) f -> p n f", p=P)
            sp.dma_start(xt[:, k * NB:NT - 1, :], xv[:, k * NB:NT - 1, :]).then_inc(x_in[1], 16)
            for s in range(G):
                sp.dma_start(rhs[W:P, s, :], w1[2 * D:2 * D + ED, :]).then_inc(weights_in, 16)
            sp.dma_start(w1_dst[:], w1[D:2 * D, :]).then_inc(weights_in, 16)
            sp.dma_start(w2_sb, w2).then_inc(weights_in, 16)
            sp.dma_start(wih_sb, w_ih).then_inc(weights_in, 16)
            sp.dma_start(whh_sb[:], w_hh).then_inc(weights_in, 16)

            def load_group(c, s):
                wait(sp, rows_in[s], c * (16 * T))
                sp.dma_start(idx[:, s, :], src_cols[bass.ds(c * (G * P) + s * P, P), :]).then_inc(idx_in[s], 16)
                wait(sp, pre_ready[s], c)
                sp.dma_start(lhs[W:P, s, :], ea_t[:, bass.ds(c * (G * GE) + s * GE, GE)]).then_inc(ea_in[s], 16)

            def chunk(c):
                for s in range(G):
                    load_group(c, s)

            def general():
                with sp.Fori(0, NT) as j:
                    sp.wait_ge(g_q_copied, j + 1)
                    sp.dma_start(q_rows[bass.ds(j * P, P), :], g_q).then_inc(g_q_stored, 16)
                with sp.Fori(0, TILES) as t:
                    sp.wait_ge(g_scattered, t * 16 + 16)
                    sp.dma_start(g_src, src_tiles[bass.ds(t, 1), :].rearrange("o p -> p o")).then_inc(g_src_in, 16)
                    sp.dma_start(g_dst, dst_tiles[bass.ds(t, 1), :].rearrange("o p -> p o")).then_inc(g_dst_in, 16)
                    sp.dma_start(lhs[W:P, 0, 0:P], ea_t[:, bass.ds(t * P, P)]).then_inc(g_ea_in, 16)
                sp.wait_ge(g_scattered, TILES * 16 + 16)

                def load_sums(j):
                    wait(sp, g_sumsT_ready, j)
                    sp.dma_start(g_sum, sum_rows[bass.ds(j * P, P), :]).then_inc(g_sums_in, 16)
                load_sums(0)
                with sp.Fori(1, NT) as j:
                    load_sums(j)
            choose(sp, lambda: over_chunks(sp, chunk), general)

        @block.gpsimd
        def _(pool):
            nc.gpsimd.memset(ident[:], 0.0).then_inc(ident_zeroed, 1)
            nc.gpsimd.memset(xt[:, NT - 1, :], 0.0).then_inc(pad_zeroed, 1)
            nc.gpsimd.memset(zero1[:], 0.0)
            nc.gpsimd.iota(iota_w[:], [[1, W]], base=0, channel_multiplier=0, allow_small_or_imprecise_dtypes=True)
            nc.gpsimd.iota(floor_c[:], [[1, 1]], base=-FN, channel_multiplier=FN, allow_small_or_imprecise_dtypes=True)
            pool.wait_ge(ident_zeroed, 1)
            nc.gpsimd.affine_select(out=ident[:], in_=ident[:], compare_op=ALU.not_equal, fill=1.0, base=0,
                                    pattern=[[-1, P]], channel_multiplier=1).then_inc(consts_ready, 1)
            pool.wait_ge(b1_in, 16)
            pv = p_rows.rearrange("(n p) f -> p n f", p=P)
            with pool.Fori(0, BATCHES // 2) as i:
                for par in range(2):
                    pool.wait_ge(p_copied[par], i + 1)
                    nc.gpsimd.tensor_tensor(stage[par], stage[par], b1_bc.unsqueeze(1).to_broadcast([P, NB, D]),
                                            ALU.add).then_inc(p_biased[par], 1)
                    pool.wait_ge(b1_in, 16)
                    pool.wait_ge(p_biased[par], i + 1)
                    pool.dma_start(pv[:, bass.ds((i * 2 + par) * NB, NB), :], stage[par]).then_inc(p_stored[par], 16)
            for par in range(2):
                pool.wait_ge(p_stored[par], BATCHES // 2 * 16)

            arrived_reg = pool.alloc_register("indices_arrived")

            def chunk(c):
                arrived = c * 16 + 16
                if not isinstance(c, int):
                    pool.reg_add(arrived_reg, c * 16, 16)
                    arrived = arrived_reg
                for s in range(G):
                    pool.wait_ge(p_stored[1], BATCHES // 2 * 16)
                    pool.wait_ge(idx_in[s], arrived)
                    wait(pool, seg_ready[s], c)
                    for t in range(T):
                        pool.indirect_dma_start(
                            out=rows[:, s, t, :], out_offset=None, in_=p_rows[:, :],
                            in_offset=bass.IndirectOffsetOnAxis(ap=idx[:, s, t:t + 1], axis=0)).then_inc(rows_in[s], 16)

            def general():
                nc.gpsimd.memset(g_zero, 0.0).then_inc(g_zeroed, 1)
                nc.gpsimd.memset(g_earlier, 1.0).then_inc(g_zeroed, 1)
                pool.wait_ge(g_zeroed, 2)
                nc.gpsimd.affine_select(out=g_earlier, in_=g_earlier, compare_op=ALU.is_gt, fill=0.0, base=0,
                                        pattern=[[-1, P]], channel_multiplier=1).then_inc(g_mask_set, 1)
                pool.wait_ge(g_q_stored, NT * 16)
                pool.dma_start(sum_rows.rearrange("(n p) f -> p n f", p=P),
                               g_zero.unsqueeze(1).to_broadcast([P, NT, ROW])).then_inc(g_scattered, 16)
                arrived = pool.alloc_register("tile_arrived")
                with pool.Fori(0, TILES) as t:
                    pool.reg_add(arrived, t * 16, 16)
                    pool.wait_ge(p_stored[1], BATCHES // 2 * 16)
                    pool.wait_ge(g_src_in, arrived)
                    pool.wait_ge(g_dst_in, arrived)
                    pool.wait_ge(g_scattered, arrived)
                    for gathered, (buffer, table, index) in zip(g_gathered, ((g_p, p_rows, g_src), (g_q, q_rows, g_dst), (g_sum, sum_rows, g_dst))):
                        pool.indirect_dma_start(out=buffer, out_offset=None, in_=table[:, :],
                                                in_offset=bass.IndirectOffsetOnAxis(ap=index, axis=0)).then_inc(gathered, 16)
                    pool.reg_add(arrived, t, 1)
                    pool.wait_ge(flag_ready, 1)
                    pool.wait_ge(g_new_ready, arrived)
                    pool.indirect_dma_start(out=sum_rows[:, :], out_offset=bass.IndirectOffsetOnAxis(ap=g_out_idx, axis=0),
                                            in_=g_new, in_offset=None, bounds_check=NPAD - 1,
                                            oob_is_err=False).then_inc(g_scattered, 16)
            choose(pool, lambda: over_chunks(pool, chunk), general)

        @block.scalar
        def _(act):
            act.dma_start(dst_nat, dst_rows).then_inc(dstn_in, 16)
            act.dma_start(dst_int[:], dst_cols).then_inc(dst_in, 16)
            act.dma_start(b1_bc, b1.unsqueeze(0).to_broadcast([P, D])).then_inc(b1_in, 16)
            act.dma_start(b2_col[:], b2.unsqueeze(1)).then_inc(bias_in, 16)
            act.dma_start(bih_col[:], b_ih).then_inc(bias_in, 16)
            act.dma_start(bhh_col[:], b_hh).then_inc(bias_in, 16)
            act.wait_ge(ranges_ready, 1)
            act.dma_start(base_f_dram, base_f[0:CHUNKS, :]).then_inc(base_stored, 16)
            act.dma_start(base_i_dram, base_n[0:CHUNKS, :]).then_inc(base_stored, 16)
            act.wait_ge(base_stored, 32)
            act.dma_start(base_i, base_i_dram.rearrange("(o c) g -> o (c g)", o=1)).then_inc(base_i_in, 16)
            act.dma_start(base_bc, base_f_dram.rearrange("(o c) g -> o (c g)", o=1).to_broadcast([P, GROUPS])).then_inc(base_bc_in, 16)

            act.wait_ge(eps_set, 1)

            def deviation(i, par):
                act.wait_ge(aggr_done[par], i + 1)
                nc.scalar.activation(std[:, par, :], mv[:, par, :, 1], ACT.Sqrt, bias=eps_col[:]).then_inc(std_ready[par], 1)

            def relu_tiles(i, par, first):
                act.wait_ge(xT_ready[par], i + 1)
                if not first:
                    act.wait_ge(p_ready[par], i)
                nc.scalar.activation(hT_batch[par], xT_ps[par], ACT.Relu).then_inc(hT_ready[par], 1)
                nc.scalar.activation(hT[:, bass.ds((i * 2 + par) * (NB * D), NB * D)], xT_ps[par], ACT.Relu).then_inc(hT_kept[par], 1)

            def copy_products(i, par, first):
                act.wait_ge(p_ready[par], i + 1)
                if not first:
                    act.wait_ge(p_stored[par], i * 16)
                nc.scalar.copy(stage[par].rearrange("p n f -> p (n f)"), p_ps[par]).then_inc(p_copied[par], 1)

            deviation(0, 0)
            deviation(0, 1)
            relu_tiles(0, 0, True)
            deviation(1, 0)
            relu_tiles(0, 1, True)
            copy_products(0, 0, True)
            deviation(1, 1)
            relu_tiles(1, 0, False)
            copy_products(0, 1, True)
            with act.Fori(1, BATCHES // 2 - 1) as i:
                deviation(i + 1, 0)
                relu_tiles(i, 1, False)
                copy_products(i, 0, False)
                deviation(i + 1, 1)
                relu_tiles(i + 1, 0, False)
                copy_products(i, 1, False)
            i = BATCHES // 2 - 1
            relu_tiles(i, 1, False)
            copy_products(i, 0, False)
            copy_products(i, 1, False)

            act.wait_ge(w2T_ready, 1)
            nc.scalar.copy(w2T, setup_ps[:, 0:D]).then_inc(w2T_copied, 1)
            act.wait_ge(w2ih_ready, 1)
            nc.scalar.copy(w2ih[:], setup_ps[:, 0:GATES]).then_inc(w2ih_copied, 1)
            act.wait_ge(w2ih_ready, 2)
            nc.scalar.copy(b2ih[:], setup_ps[0:1, 0:GATES]).then_inc(w2ih_copied, 1)
            for par in range(2):
                act.wait_ge(p_stored[par], BATCHES // 2 * 16)
            act.wait_ge(dst_rel_ready, 1)
            nc.scalar.copy(deg[0:1, 0:N], zero1[0:1, 0:1].to_broadcast([1, N])).then_inc(deg_zeroed, 1)

            act.wait_ge(base_i_in, 16)
            for par in range(2):
                act.wait_ge(hT_kept[par], BATCHES // 2)

            def copy_window(c, s):
                b = act.value_load(base_i[0:1, bass.ds(c * G + s, 1)], min_val=0, max_val=BMAX)
                old = before(c, s, 1)
                if old:
                    act.wait_ge(onehotT_ready[old[1]], old[0] + 1)
                nc.scalar.copy(h_win[:], hT[:, bass.ds(b, W)]).then_inc(h_win_ready[s], 1)

            def copy_onehot(c, s):
                act.wait_ge(onehotT_ready[s], c + 1)
                wait(act, pre_ready[s], c)
                nc.scalar.activation(lhs[0:W, s, :], onehotT_ps, ACT.Copy, accum_out=count[:, s:s + 1])
                nc.scalar.copy(rhs[0:W, s, :], q_ps).then_inc(lhs_ready[s], 1)

            def relu_message(c, s):
                act.wait_ge(summed[s], c + 1)
                m = rows[:, s, :, :]
                nc.scalar.activation(m, m, ACT.Relu).then_inc(message_ready[s], 1)

            def load_x_fin(n):
                wait(act, out_ready, n)
                act.dma_start(x_fin[:], x[bass.ds(n * FN, FN), :]).then_inc(x_fin_in, 16)

            def gate_activations(n):
                act.wait_ge(gates_ready, n + 1)
                wait(act, upd_ready, n)
                for g in range(2):
                    last = nc.scalar.activation(rz[:, g, :], gate_ps[:, g, :], ACT.Sigmoid, bias=brz_col[:, g:g + 1])
                last.then_inc(rz_ready, 1)

            def candidate(n):
                act.wait_ge(n_pre_ready, n + 1)
                nc.scalar.activation(cand[:], cand[:], ACT.Tanh, bias=bih_col[:, 2:3]).then_inc(cand_ready, 1)

            def store(n):
                act.wait_ge(out_ready, n + 1)
                act.dma_start(out[bass.ds(n * FN, FN), :], out_fin[:]).then_inc(stored, 16)

            def chunk(c):
                n, ending = finishing(c)
                for s in range(G):
                    if s == 0:
                        copy_window(c, 0)
                    copy_onehot(c, s)
                    if s + 1 < G:
                        copy_window(c, s + 1)
                    old = before(c, s, 2)
                    if old:
                        relu_message(*old)
                    if s == 1 and ending is not None:
                        store(ending)
                    if s == 2 and n is not None:
                        load_x_fin(n)
                    if s == 3 and n is not None:
                        gate_activations(n)
                    if s == 4 and n is not None:
                        candidate(n)

            def fin(n):
                load_x_fin(n)
                gate_activations(n)
                candidate(n)
                store(n)

            def fast():
                over_chunks(act, chunk)
                for back in (2, 1):
                    relu_message(CHUNKS - 1, G - back)
                store(CHUNKS - LAG - 1)
                for n in range(CHUNKS - LAG, CHUNKS):
                    fin(n)

            def general():
                def q_tile(j):
                    wait(act, g_q_ready, j)
                    nc.scalar.copy(g_bc, hT[:, bass.ds(j * P, P)]).then_inc(g_h_ready, 1)
                    wait(act, g_q_stored, j * 16)
                    act.wait_ge(g_q_ready, j + 1)
                    nc.scalar.copy(g_q, seg_ps[:, 0:D]).then_inc(g_q_copied, 1)
                q_tile(0)
                with act.Fori(1, NT) as j:
                    q_tile(j)
                with act.Fori(0, TILES) as t:
                    act.wait_ge(g_summed, t + 1)
                    nc.scalar.activation(g_p, g_p, ACT.Relu).then_inc(g_message_ready, 1)
                with act.Fori(0, NT) as j:
                    act.wait_ge(g_sumsT_ready, j + 1)
                    nc.scalar.copy(acc[:, bass.ds(j * P, P)], seg_ps[:, 0:P])
                    nc.scalar.copy(deg[0:1, bass.ds(j * P, P)], gate_ps1[0:1, 0:P]).then_inc(g_sumsT_kept, 1)
                over_fin(act, fin)
            choose(act, fast, general)
            act.wait_ge(stored, CHUNKS * 16)

        @block.vector
        def _(dve):
            chain = [0]

            def link(ins):
                chain[0] += 1
                ins.then_inc(dve_chain, 1)
                dve.wait_ge(dve_chain, chain[0])

            nc.vector.memset(eps_col[:], EPS).then_inc(eps_set, 1)
            dve.wait_ge(dstn_in, 16)
            dn = dst_nat.rearrange("c (g e) -> c g e", g=G)
            nc.vector.tensor_reduce(gmin[0:CHUNKS, :], dn, AX.X, ALU.min)
            link(nc.vector.tensor_reduce(gmax[0:CHUNKS, :], dn, AX.X, ALU.max))
            link(nc.vector.tensor_scalar(base_f[0:CHUNKS, :], gmin[0:CHUNKS, :], float(BMAX), None, ALU.min))
            nc.vector.tensor_copy(base_n[0:CHUNKS, :], base_f[0:CHUNKS, :]).then_inc(ranges_ready, 1)
            link(nc.vector.tensor_tensor(gmax[0:CHUNKS, :], gmax[0:CHUNKS, :], base_f[0:CHUNKS, :], ALU.subtract))
            nc.vector.tensor_reduce(viol[0:CHUNKS, 0:1], gmax[0:CHUNKS, :], AX.X, ALU.max)
            link(nc.vector.tensor_reduce(viol[0:CHUNKS, 1:2], gmin[0:CHUNKS, :], AX.X, ALU.min))
            nc.vector.tensor_scalar(viol[0:CHUNKS, 0:1], viol[0:CHUNKS, 0:1], float(W - 1), None, ALU.subtract)
            dve.wait_ge(consts_ready, 1)
            link(nc.vector.tensor_tensor(viol[0:CHUNKS, 1:2], floor_c[0:CHUNKS, :], viol[0:CHUNKS, 1:2], ALU.subtract))
            nc.vector.tensor_tensor(viol[0:CHUNKS, 2:3], viol[0:CHUNKS, 0:1], viol[0:CHUNKS, 1:2], ALU.max).then_inc(viol_ready, 1)
            dve.wait_ge(violT_ready, 1)
            link(nc.vector.tensor_reduce(flag_f[:], setup_ps[0:1, 0:CHUNKS], AX.X, ALU.max))
            nc.vector.tensor_scalar(flag_i[:], flag_f[:], 0.0, None, ALU.is_gt).then_inc(flag_ready, 1)

            dve.wait_ge(x_tail_in, 16)

            turn_reg = dve.alloc_register("turn")

            def statistics(i, par, first):
                turn = 1
                if not first:
                    dve.reg_add(turn_reg, i, 1)
                    turn = turn_reg
                dve.wait_ge(x_in[par], i * 16 + 16)
                for t in range(NB):
                    last = nc.vector.bn_stats(stats[:, par, t, :], acc[:, bass.ds((i * 2 + par) * (NB * D) + t * D, D)])
                last.then_inc(stats_done[par], 1)
                dve.wait_ge(x_tail_in, 16)
                dve.wait_ge(stats_done[par], turn)
                for t in range(NB):
                    last = nc.vector.bn_aggr(mv[:, par, t, :], stats[:, par, t, :])
                last.then_inc(aggr_done[par], 1)

            def normalise(i, par, first):
                dve.wait_ge(std_ready[par], i + 1)
                nc.vector.reciprocal(rstd[:, par, :], std[:, par, :]).then_inc(rstd_done[par], 1)
                dve.wait_ge(rstd_done[par], i + 1)
                if not first:
                    dve.wait_ge(xT_ready[par], i)
                for t in range(NB):
                    last = nc.vector.tensor_scalar(xn[par][:, t * D:(t + 1) * D],
                                                   acc[:, bass.ds((i * 2 + par) * (NB * D) + t * D, D)],
                                                   mv[:, par, t, 0:1], rstd[:, par, t:t + 1], ALU.subtract, ALU.mult)
                last.then_inc(xn_ready[par], 1)

            statistics(0, 0, True)
            statistics(0, 1, True)
            normalise(0, 0, True)
            statistics(1, 0, False)
            normalise(0, 1, True)
            with dve.Fori(1, BATCHES // 2 - 1) as i:
                statistics(i, 1, False)
                normalise(i, 0, False)
                statistics(i + 1, 0, False)
                normalise(i, 1, False)
            i = BATCHES // 2 - 1
            statistics(i, 1, False)
            normalise(i, 0, False)
            normalise(i, 1, False)

            dve.wait_ge(bias_in, 48)
            nc.vector.tensor_tensor(brz_col[:], bih_col[:, 0:2], bhh_col[:, 0:2], ALU.add)
            dve.wait_ge(base_bc_in, 16)
            dve.wait_ge(base_i_in, 16)
            dve.wait_ge(dst_in, 16)
            dr = dst_rel.rearrange("p (g t) -> p g t", t=T)
            nc.vector.tensor_tensor(dr, dst_int[:, :].rearrange("p (g t) -> p g t", t=T),
                                    base_bc.unsqueeze(2).to_broadcast([P, GROUPS, T]), ALU.subtract).then_inc(dst_rel_ready, 1)
            dve.wait_ge(dst_rel_ready, 1)

            def build_onehot(c, s):
                wait(dve, seg_ready[s], c)
                d = dst_rel[:, bass.ds(c * (G * T) + s * T, T)]
                nc.vector.tensor_tensor(onehot[:, s, :, :], iota_w[:, :].unsqueeze(1).to_broadcast([P, T, W]),
                                        d.unsqueeze(2).to_broadcast([P, T, W]), ALU.is_equal).then_inc(onehot_ready[s], 1)

            def add_pre(c, s):
                dve.wait_ge(pre_ready[s], c + 1)
                dve.wait_ge(rows_in[s], c * (16 * T) + 16 * T)
                r = rows[:, s, :, :].rearrange("p t f -> p (t f)")
                nc.vector.tensor_tensor(r, r, pre_ps[s % 2], ALU.add).then_inc(summed[s], 1)

            def add_segments(c, s, prev):
                b = dve.value_load(base_i[0:1, bass.ds(c * G + s, 1)], min_val=0, max_val=BMAX)
                dve.wait_ge(seg_ready[s], c + 1)
                if prev:
                    dve.wait_ge(acc_added[prev[1]], prev[0] * 2 + 2)
                sg = seg_ps
                nc.vector.tensor_tensor(acc[:, bass.ds(b, W)], acc[:, bass.ds(b, W)], sg[:, 0:W], ALU.add).then_inc(acc_added[s], 1)
                nc.vector.tensor_tensor(deg[0:1, bass.ds(b, W)], deg[0:1, bass.ds(b, W)], sg[0:1, W:2 * W],
                                        ALU.add).then_inc(acc_added[s], 1)

            def candidate_pre(n):
                dve.wait_ge(rz_ready, n + 1)
                nc.vector.scalar_tensor_tensor(out=upd[:], in0=gate_ps[:, 3, :], scalar=bhh_col[:, 2:3], in1=rz[:, 0, :],
                                               op0=ALU.add, op1=ALU.mult).then_inc(fin_chain, 1)
                dve.wait_ge(fin_chain, n * 3 + 1)
                nc.vector.tensor_tensor(cand[:], upd[:], gate_ps[:, 2, :], ALU.add).then_inc(n_pre_ready, 1)

            def update(n):
                dve.wait_ge(cand_ready, n + 1)
                h = hT[:, bass.ds(n * FN, FN)]
                nc.vector.tensor_tensor(upd[:], h, cand[:], ALU.subtract).then_inc(fin_chain, 1)
                dve.wait_ge(fin_chain, n * 3 + 2)
                nc.vector.tensor_tensor(upd[:], upd[:], rz[:, 1, :], ALU.mult).then_inc(fin_chain, 1)
                dve.wait_ge(fin_chain, n * 3 + 3)
                nc.vector.tensor_tensor(upd[:], upd[:], cand[:], ALU.add).then_inc(upd_ready, 1)

            def residual(n):
                dve.wait_ge(back_ready, n + 1)
                dve.wait_ge(x_fin_in, n * 16 + 16)
                wait(dve, stored, n * 16)
                nc.vector.tensor_tensor(out_fin[:], x_fin[:], back_ps, ALU.add).then_inc(out_ready, 1)

            def chunk(c):
                n, ending = finishing(c)
                for s in range(G):
                    build_onehot(c, s)
                    old = before(c, s, 2)
                    if old:
                        add_pre(*old)
                    old = before(c, s, 3)
                    if old:
                        if isinstance(c, int) and c == 0 and s == 3:
                            dve.wait_ge(deg_zeroed, 1)
                        add_segments(*old, before(c, s, 4))
                    if isinstance(c, int) and c == 0 and s == 0:
                        nc.vector.memset(acc[:, 0:N], 0.0).then_inc(acc_zeroed, 1)
                        dve.wait_ge(acc_zeroed, 1)
                    if s == 0 and ending is not None:
                        residual(ending)
                    if s == 3 and n is not None:
                        candidate_pre(n)
                    if s == 4 and n is not None:
                        update(n)

            def fin(n):
                candidate_pre(n)
                update(n)
                residual(n)

            def fast():
                over_chunks(dve, chunk)
                residual(CHUNKS - LAG - 1)
                c = CHUNKS - 1
                add_pre(c, G - 2)
                add_segments(c, G - 3, (c, G - 4))
                add_pre(c, G - 1)
                add_segments(c, G - 2, (c, G - 3))
                add_segments(c, G - 1, (c, G - 2))
                for n in range(CHUNKS - LAG, CHUNKS):
                    fin(n)

            def general():
                dve.wait_ge(g_mask_set, 1)
                dve.wait_ge(g_q_stored, NT * 16)
                nc.vector.memset(g_new, 0.0)
                with dve.Fori(0, TILES) as t:
                    step = [0]
                    steps = 8

                    def then(ins):
                        step[0] += 1
                        ins.then_inc(g_chain, 1)
                        dve.wait_ge(g_chain, t * steps + step[0])

                    dve.wait_ge(g_dst_in, t * 16 + 16)
                    then(nc.vector.tensor_copy(g_dstf, g_dst))
                    nc.vector.tensor_copy(g_bc, g_dstf.to_broadcast([P, P])).then_inc(g_bc_ready, 1)
                    dve.wait_ge(g_bcT_ready, t + 1)
                    then(nc.vector.tensor_scalar(g_eq, g_dst_ps, g_dstf, None, ALU.is_equal))
                    then(nc.vector.tensor_reduce(g_count, g_eq, AX.X, ALU.add))
                    then(nc.vector.tensor_tensor(g_dup, g_eq, g_earlier, ALU.mult))
                    then(nc.vector.tensor_reduce(g_isdup, g_dup, AX.X, ALU.max))
                    then(nc.vector.scalar_tensor_tensor(out=g_outf, in0=g_isdup, scalar=float(2 * NPAD), in1=g_dstf,
                                                        op0=ALU.mult, op1=ALU.add))
                    then(nc.vector.tensor_copy(g_out_idx, g_outf))
                    dve.wait_ge(g_pre_ready, t + 1)
                    for gathered in g_gathered:
                        dve.wait_ge(gathered, t * 16 + 16)
                    then(nc.vector.tensor_tensor(g_p, g_p, pre_ps[0][:, 0:D], ALU.add))
                    assert step[0] == steps
                    nc.vector.tensor_tensor(g_p, g_p, g_q, ALU.add).then_inc(g_summed, 1)
                    nc.vector.tensor_tensor(g_new[:, D:D + 1], g_sum[:, D:D + 1], g_count, ALU.add)
                    dve.wait_ge(g_seg_ready, t + 1)
                    nc.vector.tensor_tensor(g_new[:, 0:D], g_sum[:, 0:D], seg_ps[:, 0:D], ALU.add).then_inc(g_new_ready, 1)
                over_fin(dve, fin)

            for par in range(2):
                dve.wait_ge(xT_ready[par], BATCHES // 2)
            choose(dve, fast, general)

        @block.tensor
        def _(pe):
            pe.wait_ge(consts_ready, 1)
            pe.wait_ge(viol_ready, 1)
            nc.tensor.transpose(setup_ps[0:1, 0:CHUNKS], viol[0:CHUNKS, 2:3], ident[0:CHUNKS, 0:CHUNKS]).then_inc(violT_ready, 1)
            pe.wait_ge(flag_ready, 1)
            pe.wait_ge(w1_in, 16)

            def transpose_rows(i, par, first):
                pe.wait_ge(xn_ready[par], i + 1)
                if not first:
                    pe.wait_ge(hT_kept[par], i)
                for t in range(NB):
                    last = nc.tensor.transpose(xT_ps[par][:, t * D:(t + 1) * D], xn[par][:, t * D:(t + 1) * D], ident[:])
                last.then_inc(xT_ready[par], 1)

            def products(i, par, first):
                pe.wait_ge(hT_ready[par], i + 1)
                if not first:
                    pe.wait_ge(p_copied[par], i)
                for t in range(NB):
                    last = nc.tensor.matmul(p_ps[par][:, t * D:(t + 1) * D], hT_batch[par][:, t * D:(t + 1) * D], w1_src,
                                            start=True, stop=True)
                last.then_inc(p_ready[par], 1)

            transpose_rows(0, 0, True)
            transpose_rows(0, 1, True)
            products(0, 0, True)
            transpose_rows(1, 0, False)
            products(0, 1, True)
            with pe.Fori(1, BATCHES // 2 - 1) as i:
                transpose_rows(i, 1, False)
                products(i, 0, False)
                transpose_rows(i + 1, 0, False)
                products(i, 1, False)
            i = BATCHES // 2 - 1
            transpose_rows(i, 1, False)
            products(i, 0, False)
            products(i, 1, False)

            for par in range(2):
                pe.wait_ge(hT_kept[par], BATCHES // 2)
                pe.wait_ge(p_copied[par], BATCHES // 2)
            pe.wait_ge(weights_in, 16 * (G + 4))
            nc.tensor.transpose(setup_ps[:, 0:D], w2_sb, ident[:]).then_inc(w2T_ready, 1)
            pe.wait_ge(w2T_copied, 1)
            nc.tensor.matmul(setup_ps[:, 0:GATES], w2T, wih_sb, start=True, stop=True).then_inc(w2ih_ready, 1)
            pe.wait_ge(w2ih_copied, 1)
            pe.wait_ge(bias_in, 48)
            nc.tensor.matmul(setup_ps[0:1, 0:GATES], b2_col[:], wih_sb, start=True, stop=True).then_inc(w2ih_ready, 1)
            pe.wait_ge(w2ih_copied, 2)

            def transpose_onehot(c, s):
                pe.wait_ge(onehot_ready[s], c + 1)
                old = before(c, s, 1)
                if old:
                    pe.wait_ge(lhs_ready[old[1]], old[0] + 1)
                for t in range(T):
                    nc.tensor.transpose(onehotT_ps[:, t * P:(t + 1) * P], onehot[:, s, t, :], ident[:])
                pe.wait_ge(h_win_ready[s], c + 1)
                nc.tensor.matmul(q_ps, h_win[:], w1_dst[:], start=True, stop=True).then_inc(onehotT_ready[s], 1)

            def pre_activation(c, s):
                old = before(c, s, {0: 1, 1: 3}.get(s, 2))
                if old:
                    pe.wait_ge(summed[old[1]], old[0] + 1)
                pe.wait_ge(lhs_ready[s], c + 1)
                pe.wait_ge(ea_in[s], c * 16 + 16)
                for t in range(T):
                    last = nc.tensor.matmul(pre_ps[s % 2][:, t * D:(t + 1) * D], lhs[:, s, t * P:(t + 1) * P],
                                            rhs[:, s, :], start=True, stop=True)
                last.then_inc(pre_ready[s], 1)

            def segment_sums(c, s):
                pe.wait_ge(message_ready[s], c + 1)
                old = before(c, s, 1)
                if old:
                    pe.wait_ge(acc_added[old[1]], old[0] * 2 + 2)
                sg = seg_ps
                for t in range(T):
                    nc.tensor.matmul(sg[:, 0:W], rows[:, s, t, :], onehot[:, s, t, :], start=(t == 0), stop=(t == T - 1))
                nc.tensor.transpose(sg[0:1, W:2 * W], count[:, s:s + 1], ident[0:W, 0:W]).then_inc(seg_ready[s], 1)

            def gates(n):
                if not (isinstance(n, int) and n == 0):
                    wait(pe, out_ready, n)
                a, d, h = (v[:, bass.ds(n * FN, FN)] for v in (acc, deg, hT))
                for g in range(3):
                    cols = slice(g * D, (g + 1) * D)
                    nc.tensor.matmul(gate_ps[:, g, :], w2ih[:, cols], a, start=True, stop=False)
                    last = nc.tensor.matmul(gate_ps[:, g, :], b2ih[0:1, cols], d, start=False, stop=(g == 2))
                    if g < 2:
                        nc.tensor.matmul(gate_ps[:, g, :], whh_sb[:, cols], h, start=False, stop=True)
                nc.tensor.matmul(gate_ps[:, 3, :], whh_sb[:, 2 * D:3 * D], h, start=True, stop=True).then_inc(gates_ready, 1)

            def back(n):
                pe.wait_ge(upd_ready, n + 1)
                nc.tensor.transpose(back_ps, upd[:], ident[:]).then_inc(back_ready, 1)

            def chunk(c):
                n, ending = finishing(c)
                for s in range(G):
                    transpose_onehot(c, s)
                    old = before(c, s, 1)
                    if old:
                        pre_activation(*old)
                    old = before(c, s, 2)
                    if old:
                        segment_sums(*old)
                    if s == 0 and ending is not None:
                        back(ending)
                    if s == 2 and n is not None:
                        pe.wait_ge(acc_added[G - 1], c * 2)
                        gates(n)

            def fin(n):
                gates(n)
                back(n)

            def fast():
                over_chunks(pe, chunk)
                back(CHUNKS - LAG - 1)
                c = CHUNKS - 1
                pre_activation(c, G - 1)
                segment_sums(c, G - 2)
                segment_sums(c, G - 1)
                pe.wait_ge(acc_added[G - 1], CHUNKS * 2)
                for n in range(CHUNKS - LAG, CHUNKS):
                    fin(n)

            def general():
                def q_tile(j):
                    pe.wait_ge(g_h_ready, j + 1)
                    wait(pe, g_q_copied, j)
                    nc.tensor.matmul(seg_ps[:, 0:D], g_bc, w1_dst[:], start=True, stop=True).then_inc(g_q_ready, 1)
                q_tile(0)
                with pe.Fori(1, NT) as j:
                    q_tile(j)
                with pe.Fori(0, TILES) as t:
                    pe.wait_ge(g_bc_ready, t + 1)
                    nc.tensor.transpose(g_dst_ps, g_bc, ident[:]).then_inc(g_bcT_ready, 1)
                    pe.wait_ge(g_ea_in, t * 16 + 16)
                    nc.tensor.matmul(pre_ps[0][:, 0:D], lhs[W:P, 0, 0:P], rhs[W:P, 0, :], start=True,
                                     stop=True).then_inc(g_pre_ready, 1)
                    pe.wait_ge(g_message_ready, t + 1)
                    nc.tensor.matmul(seg_ps[:, 0:D], g_eq, g_p, start=True, stop=True).then_inc(g_seg_ready, 1)

                def transpose_sums(j):
                    pe.wait_ge(g_sums_in, j * 16 + 16)
                    wait(pe, g_sumsT_kept, j)
                    nc.tensor.transpose(seg_ps[:, 0:P], g_sum[:, 0:D], ident[:])
                    nc.tensor.transpose(gate_ps1, g_sum[:, D:D + 1], ident[:]).then_inc(g_sumsT_ready, 1)
                transpose_sums(0)
                with pe.Fori(1, NT) as j:
                    transpose_sums(j)
                pe.wait_ge(g_sumsT_kept, NT)
                over_fin(pe, fin)
            choose(pe, fast, general)


_OUTS = [((N, D), "float32")]


def kernel(**inputs):
    import numpy as _np
    import concourse.bacc as _bacc
    from concourse import mybir as _mybir
    from concourse.bass_utils import run_bass_kernel_spmd as _run

    src = _np.asarray(inputs["src"])
    dst = _np.asarray(inputs["dst"])
    w = {k: _np.ascontiguousarray(inputs["L0_gnn_" + k]) for k in ("w1", "b1", "w2", "b2", "w_ih", "b_ih", "w_hh", "b_hh")}
    for k in ("b_ih", "b_hh"):
        w[k] = _np.ascontiguousarray(w[k].reshape(3, D).T)
    laid = {
        "x": _np.ascontiguousarray(inputs["x"]),
        "src_cols": _np.ascontiguousarray(src.reshape(GROUPS, T, P).transpose(0, 2, 1).reshape(GROUPS * P, T)),
        "dst_cols": _np.ascontiguousarray(dst.reshape(GROUPS * T, P).T),
        "dst_rows": _np.ascontiguousarray(dst.reshape(CHUNKS, G * GE)),
        "src_tiles": _np.ascontiguousarray(src.reshape(TILES, P)),
        "dst_tiles": _np.ascontiguousarray(dst.reshape(TILES, P)),
        "ea_t": _np.ascontiguousarray(_np.asarray(inputs["edge_attr_32"]).T),
        **w,
    }
    nc = _bacc.Bacc("TRN2", target_bir_lowering=False, num_devices=1)
    arrays, args = {}, []
    for name, a in laid.items():
        arrays[f"in_{name}_dram"] = a
        args.append(nc.dram_tensor(f"in_{name}_dram", a.shape, _mybir.dt.from_np(a.dtype), kind="ExternalInput").ap())
    for i, (shape, dtype) in enumerate(_OUTS):
        dt = _mybir.dt.from_np(_np.dtype(dtype))
        args.append(nc.dram_tensor(f"out_{i}_dram", shape, dt, kind="ExternalOutput").ap())
    gnn_kernel(nc, *args)
    r = _run(nc, [arrays], core_ids=[0])
    return r.results[0]["out_0_dram"]
```

```python
from contextlib import ExitStack

import concourse.bass as bass
from concourse import mybir

ALU = mybir.AluOpType
ACT = mybir.ActivationFunctionType
AX = mybir.AxisListType
F32 = mybir.dt.float32
I32 = mybir.dt.int32

P = 128
EPS = 1e-05

N = 12500
NT = -(-N // P)
NPAD = NT * P
NB = 7
LOADS_AHEAD = 4
DST_PARTS = LOADS_AHEAD + 1
POOL_FROM = 2
ACT_FROM = 6
BATCHES = NT // NB
TAIL = N - (NT - 1) * P
assert BATCHES % 2 == 0 and BATCHES * NB == NT

E = 400000
T = 5
G = 5
GE = T * P
GROUPS = E // GE
CHUNKS = GROUPS // G
TILES = GROUPS * T
assert CHUNKS * G * GE == E

ED = 32
WB = P - ED
W = WB - 1
BMAX = N - W
FN = N // CHUNKS
assert FN * CHUNKS == N
LAG = 2
LN = LAG * FN
N_ZERO_DVE = N // 3

D = 128
GATES = 3 * D
ROW = D + 4


def gnn_kernel(nc, x, src_cols, dst_cols, dst_rows, src_tiles, dst_tiles, ea_t, w1, b1, w2, b2, w_ih, b_ih, w_hh, b_hh, out):
    p_rows = nc.dram_tensor("p_rows", [NPAD, D], F32, kind="Internal").ap()
    base_f_dram = nc.dram_tensor("base_f_dram", [CHUNKS, G], F32, kind="Internal").ap()
    base_i_dram = nc.dram_tensor("base_i_dram", [CHUNKS, G], I32, kind="Internal").ap()

    q_rows = nc.dram_tensor("q_rows", [NPAD, D], F32, kind="Internal").ap()
    sum_rows = nc.dram_tensor("sum_rows", [NPAD, ROW], F32, kind="Internal").ap()

    with ExitStack() as ctx:
        def sb(name, shape, dt=F32):
            return ctx.enter_context(nc.sbuf_tensor(name, shape, dt))

        def sem(name):
            return ctx.enter_context(nc.semaphore(name))

        def sems(name, n):
            return [sem(f"{name}{i}") for i in range(n)]

        acc = sb("acc", [P, NPAD])
        xt = acc[:, :].rearrange("p (n f) -> p n f", f=D)
        hT = sb("hT", [P, NPAD])
        low = sb("low", [P, NPAD])
        deg = low[0:1, :]
        SW = NB * D
        stage = [low[:, k * SW:(k + 1) * SW].rearrange("p (n f) -> p n f", f=D) for k in range(2)]
        at = 2 * SW
        dst_nat = low[0:CHUNKS, at:at + G * GE].bitcast(I32)
        at += G * GE
        w1_src = low[:, at:at + D]
        at += D
        w2_sb = low[:, at:at + D]
        at += D
        w2T = low[:, at:at + D]
        at += D
        wih_sb = low[:, at:at + GATES]
        at += GATES
        xn = [low[:, at + k * NB * D:at + (k + 1) * NB * D] for k in range(2)]
        at += 2 * NB * D
        hT_batch = [low[:, at + k * NB * D:at + (k + 1) * NB * D] for k in range(2)]
        at += 2 * NB * D
        base_i = low[ED:ED + 1, at:at + GROUPS].bitcast(I32)
        at += GROUPS
        assert at <= NPAD

        dst_int = sb("dst_int", [P, GROUPS * T], I32)
        dst_rel = dst_int[:, :].bitcast(F32)
        rows = sb("rows", [P, G, T, D])
        onehot = sb("onehot", [P, G, T, WB])
        base_bc = onehot[:, :, :, :].rearrange("p g t w -> p (g t w)")[:, 0:GROUPS]
        lhs = sb("lhs", [P, G, GE])
        rhs = sb("rhs", [P, G, D])
        h_win = sb("h_win", [P, W])
        w1_dst = sb("w1_dst", [P, D])
        idx = sb("idx", [P, G, T], I32)
        count = sb("count", [WB, G])
        ident = sb("ident", [P, P])
        iota_w = sb("iota_w", [P, W])
        w2ih = sb("w2ih", [P, GATES])
        whh_sb = sb("whh_sb", [P, GATES])
        b2_col = sb("b2_col", [P, 1])
        b2ih = sb("b2ih", [1, GATES])
        bih_col = sb("bih_col", [P, 3])
        bhh_col = sb("bhh_col", [P, 3])
        brz_col = sb("brz_col", [P, 2])
        eps_col = sb("eps_col", [P, 1])
        stats = sb("stats", [P, 2, NB, 6])
        mv = sb("mv", [P, 2, NB, 2])
        std = sb("std", [P, 2, NB])
        rstd = sb("rstd", [P, 2, NB])
        table_load = sb("table_load", [P, 1])
        zero_col = sb("zero_col", [P, 1])
        shift = sb("shift", [P, 2, NB])
        gmin = sb("gmin", [P, G])
        gmax = sb("gmax", [P, G])
        base_f = sb("base_f", [P, G])
        base_n = sb("base_n", [P, G], I32)
        viol = sb("viol", [P, 4])
        floor_c = sb("floor_c", [P, 1])
        flag_f = sb("flag_f", [1, 1])
        flag_i = sb("flag_i", [1, 1], I32)
        rz = sb("rz", [P, 2, FN])
        cand = sb("cand", [P, FN])
        upd = sb("upd", [P, FN])
        x_fin = sb("x_fin", [FN, D])
        out_fin = sb("out_fin", [FN, D])

        last_rz = rows[:, 0, :, :].rearrange("p t f -> p (t f)")[:, 0:2 * LN].rearrange("p (g n) -> p g n", g=2)
        last_cand = rows[:, 0, :, :].rearrange("p t f -> p (t f)")[:, 2 * LN:3 * LN]
        last_upd = rows[:, 1, 0:2, :].rearrange("p t f -> p (t f)")[:, 0:LN]
        last_x = rows[0:FN, 1, 2:2 + LAG, :]
        last_out = rows[0:FN, 2, 0:LAG, :]

        g_src, g_dst, g_out_idx = (idx[:, 0, k:k + 1] for k in range(3))
        g_p, g_q = rows[:, 0, 0, :], rows[:, 0, 1, :]
        g_sum, g_new = (rows[:, k, 0:2, :].rearrange("p t f -> p (t f)")[:, 0:ROW] for k in (1, 2))
        g_bc, g_eq, g_dup = (rows[:, 3, k, :] for k in range(3))
        g_earlier = rows[:, 4, 0, :]
        g_zero = rows[:, 4, 1:3, :].rearrange("p t f -> p (t f)")[:, 0:ROW]
        g_b1, g_one = rhs[0:1, 0, :], lhs[0:1, 0, 0:P]
        g_cols = sb("g_cols", [P, 4])
        g_dstf, g_count, g_isdup, g_outf = (g_cols[:, k:k + 1] for k in range(4))

        ps = ctx.enter_context(nc.psum_tensor("ps", [P, 4096], F32))
        onehotT_ps = ps[0:WB, 0:GE]
        pre_ps = [ps[:, 1024 + k * 1024:1024 + k * 1024 + GE] for k in range(2)]
        seg_ps = ps[:, 3072:3072 + 2 * W]
        g_dst_ps = ps[:, 0:P]
        gate_ps = ps[:, 3584:3584 + 4 * FN].rearrange("p (g n) -> p g n", g=4)
        back_ps = ps[0:FN, 3584:3584 + D]
        gate_ps1 = ps[0:1, 3584:3584 + P]
        q_ps = ps[0:W, GE:GE + D]
        last_ps = [ps[:, b * 512:b * 512 + LN] for b in (0, 1, 2, 4)]
        last_back = ps[0:FN, 3584:3584 + LAG * D].rearrange("p (k f) -> p k f", k=LAG)
        xT_ps = [ps[:, k * 1024:k * 1024 + NB * D] for k in range(2)]
        p_ps = [ps[:, 2048 + k * 1024:2048 + k * 1024 + NB * D] for k in range(2)]
        setup_ps = ps[:, 0:512]
        violT_ps = ps[0:1, 4096 - P:4096 - P + CHUNKS]

        w1_in, weights_in, bias_in, dst_in, dstn_in = (sem(n) for n in ("w1_in", "weights_in", "bias_in", "dst_in", "dstn_in"))
        ident_zeroed, consts_ready, ranges_ready, viol_ready, violT_ready, flag_ready = (sem(n) for n in (
            "ident_zeroed", "consts_ready", "ranges_ready", "viol_ready", "violT_ready", "flag_ready"))
        base_stored, base_bc_in, base_i_in, eps_set, dve_chain = (sem(n) for n in ("base_stored", "base_bc_in", "base_i_in", "eps_set", "dve_chain"))
        w2T_ready, w2T_copied, w2ih_ready, w2ih_copied = (sem(n) for n in ("w2T_ready", "w2T_copied", "w2ih_ready", "w2ih_copied"))
        pad_zeroed, x_tail_in = sem("pad_zeroed"), sem("x_tail_in")
        x_in = sems("x_in", 2)
        stats_done, aggr_done, std_ready, rstd_done, shift_ready = (sems(n, 2) for n in (
            "stats_done", "aggr_done", "std_ready", "rstd_done", "shift_ready"))
        scaled, xn_dve_ready, xn_pool_ready, xn_act_ready, xT_ready, hT_ready, hT_kept = (sems(n, 2) for n in (
            "scaled", "xn_dve_ready", "xn_pool_ready", "xn_act_ready", "xT_ready", "hT_ready", "hT_kept"))
        p_ready, p_copied, p_stored = (sems(n, 2) for n in ("p_ready", "p_copied", "p_stored"))
        dst_rel_ready, ones_set, acc_zeroed, deg_zeroed = (sem(n) for n in ("dst_rel_ready", "ones_set", "acc_zeroed", "deg_zeroed"))
        idx_in, ea_in, rows_in, h_win_ready = (sems(n, G) for n in ("idx_in", "ea_in", "rows_in", "h_win_ready"))
        onehot_ready, onehotT_ready, lhs_ready, pre_ready = (sems(n, G) for n in ("onehot_ready", "onehotT_ready", "lhs_ready", "pre_ready"))
        summed, message_ready, seg_ready, acc_added = (sems(n, G) for n in ("summed", "message_ready", "seg_ready", "acc_added"))
        gates_ready, rz_ready, n_pre_ready, cand_ready, upd_ready, back_ready, out_ready, x_fin_in, stored = (sem(n) for n in (
            "gates_ready", "rz_ready", "n_pre_ready", "cand_ready", "upd_ready", "back_ready", "out_ready", "x_fin_in", "stored"))
        fin_chain = sem("fin_chain")
        g_zeroed, g_mask_set, g_scattered, g_chain, g_b1_in = (sem(n) for n in ("g_zeroed", "g_mask_set", "g_scattered", "g_chain", "g_b1_in"))
        g_h_ready, g_q_ready, g_q_copied, g_q_stored = (sem(n) for n in ("g_h_ready", "g_q_ready", "g_q_copied", "g_q_stored"))
        g_src_in, g_dst_in, g_ea_in = (sem(n) for n in ("g_src_in", "g_dst_in", "g_ea_in"))
        g_gathered = sems("g_gathered", 3)
        g_bc_ready, g_bcT_ready, g_pre_ready, g_summed, g_message_ready, g_seg_ready, g_new_ready = (sem(n) for n in (
            "g_bc_ready", "g_bcT_ready", "g_pre_ready", "g_summed", "g_message_ready", "g_seg_ready", "g_new_ready"))
        g_sums_in, g_sumsT_ready, g_sumsT_kept = (sem(n) for n in ("g_sums_in", "g_sumsT_ready", "g_sumsT_kept"))

        block = ctx.enter_context(nc.Block())

        def wait(eng, s, value):
            if not (isinstance(value, int) and value <= 0):
                eng.wait_ge(s, value)

        def before(c, s, back):
            c2, s2 = (c, s - back) if s >= back else (c - 1, s - back + G)
            return None if isinstance(c, int) and c2 < 0 else (c2, s2)

        def over_chunks(eng, body, first=0):
            for c in range(first, LAG + 2):
                body(c)
            with eng.Fori(LAG + 2, CHUNKS) as c:
                body(c)

        def finishing(c):
            known = isinstance(c, int)
            return (c - LAG if not known or c >= LAG else None, c - LAG - 1 if not known or c > LAG else None)

        def over_fin(eng, body):
            body(0)
            with eng.Fori(1, CHUNKS) as n:
                body(n)

        def choose(eng, fast, general):
            eng.wait_ge(flag_ready, 1)
            misfit = eng.value_load(flag_i[0:1, 0:1], min_val=0, max_val=1)
            with eng.If(misfit == 0):
                fast()
            with eng.Else():
                general()

        @block.sync
        def _(sp):
            def load_x(k, par):
                xv = x[0:(NT - 1) * P, :].rearrange("(n p) f -> p n f", p=P)
                sp.dma_start(xt[:, bass.ds(k * NB, NB), :], xv[:, bass.ds(k * NB, NB), :]).then_inc(x_in[par], 16)

            pv = p_rows.rearrange("(n p) f -> p n f", p=P)

            def store(i, par):
                sp.wait_ge(p_copied[par], i + 1)
                sp.dma_start(pv[:, bass.ds((i * 2 + par) * NB, NB), :], stage[par]).then_inc(p_stored[par], 16)

            def load_next(i, par):
                sp.wait_ge(x_in[par], i * 16)
                load_x(i * 2 + par, par)

            load_x(0, 0)
            load_x(1, 1)
            sp.dma_start(w1_src, w1[0:D, :]).then_inc(w1_in, 16)
            for i in range(1, LOADS_AHEAD):
                for par in range(2):
                    load_next(i, par)
            sp.wait_ge(pad_zeroed, 1)
            sp.dma_start(xt[0:TAIL, NT - 1, :], x[(NT - 1) * P:N, :]).then_inc(x_tail_in, 16)
            sp.dma_start(rhs[WB:P, :, :], w1[2 * D:2 * D + ED, :].unsqueeze(1).to_broadcast([ED, G, D])).then_inc(weights_in, 16)
            sp.dma_start(rhs[W:WB, :, :], b1.unsqueeze(0).unsqueeze(0).to_broadcast([1, G, D])).then_inc(weights_in, 16)
            sp.dma_start(w1_dst[:], w1[D:2 * D, :]).then_inc(weights_in, 16)
            sp.dma_start(w2_sb, w2).then_inc(weights_in, 16)
            sp.dma_start(wih_sb, w_ih).then_inc(weights_in, 16)
            sp.dma_start(whh_sb[:], w_hh).then_inc(weights_in, 16)
            sp.dma_start(dst_nat, dst_rows).then_inc(dstn_in, 16)
            turns = BATCHES // 2 - LOADS_AHEAD
            with sp.Fori(0, turns - 1) as i:
                for par in range(2):
                    load_next(i + LOADS_AHEAD, par)
                    store(i, par)
            i = turns - 1
            load_next(i + LOADS_AHEAD, 0)
            store(i, 0)
            k = BATCHES - 1
            sp.wait_ge(x_in[1], k // 2 * 16)
            xv = x[0:(NT - 1) * P, :].rearrange("(n p) f -> p n f", p=P)
            sp.dma_start(xt[:, k * NB:NT - 1, :], xv[:, k * NB:NT - 1, :]).then_inc(x_in[1], 16)
            store(i, 1)

            def load_indices(c, s):
                wait(sp, rows_in[s], c * (16 * T))
                sp.dma_start(idx[:, s, :], src_cols[bass.ds(c * (G * P) + s * P, P), :]).then_inc(idx_in[s], 16)

            for s in range(G):
                load_indices(0, s)
            part = GROUPS * T // DST_PARTS
            assert part * DST_PARTS == GROUPS * T

            def load_dst(k):
                sp.dma_start(dst_int[:, bass.ds(k * part, part)], dst_cols[:, bass.ds(k * part, part)]).then_inc(dst_in, 16)

            load_dst(0)
            with sp.Fori(turns, BATCHES // 2) as i:
                for par in range(2):
                    store(i, par)
                load_dst(i - (turns - 1))

            def load_group(c, s):
                if not (isinstance(c, int) and c == 0):
                    load_indices(c, s)
                wait(sp, pre_ready[s], c)
                sp.dma_start(lhs[WB:P, s, :], ea_t[:, bass.ds(c * (G * GE) + s * GE, GE)]).then_inc(ea_in[s], 16)

            def chunk(c):
                for s in range(G):
                    load_group(c, s)
                if isinstance(c, int) and c == 0:
                    sp.wait_ge(acc_zeroed, 2)
                    for par in range(2):
                        sp.wait_ge(p_stored[par], BATCHES // 2 * 16)
                        sp.wait_ge(hT_kept[par], BATCHES // 2)
                    sp.dma_start(deg[0:1, 0:N], acc[0:1, 0:N]).then_inc(deg_zeroed, 16)

            def general():
                for s in range(G):
                    sp.wait_ge(rows_in[s], 16 * T)
                sp.dma_start(g_b1, b1.unsqueeze(0)).then_inc(g_b1_in, 16)
                with sp.Fori(0, NT) as j:
                    sp.wait_ge(g_q_copied, j + 1)
                    sp.dma_start(q_rows[bass.ds(j * P, P), :], g_q).then_inc(g_q_stored, 16)
                with sp.Fori(0, TILES) as t:
                    sp.wait_ge(g_scattered, t * 16 + 16)
                    sp.dma_start(g_src, src_tiles[bass.ds(t, 1), :].rearrange("o p -> p o")).then_inc(g_src_in, 16)
                    sp.dma_start(g_dst, dst_tiles[bass.ds(t, 1), :].rearrange("o p -> p o")).then_inc(g_dst_in, 16)
                    sp.dma_start(lhs[WB:P, 0, 0:P], ea_t[:, bass.ds(t * P, P)]).then_inc(g_ea_in, 16)
                sp.wait_ge(g_scattered, TILES * 16 + 16)

                def load_sums(j):
                    wait(sp, g_sumsT_ready, j)
                    sp.dma_start(g_sum, sum_rows[bass.ds(j * P, P), :]).then_inc(g_sums_in, 16)
                load_sums(0)
                with sp.Fori(1, NT) as j:
                    load_sums(j)
            choose(sp, lambda: over_chunks(sp, chunk), general)

        @block.gpsimd
        def _(pool):
            nc.gpsimd.memset(ident[:], 0.0).then_inc(ident_zeroed, 1)
            nc.gpsimd.memset(xt[:, NT - 1, :], 0.0).then_inc(pad_zeroed, 1)
            nc.gpsimd.memset(zero_col[:], 0.0)
            nc.gpsimd.iota(iota_w[:], [[1, W]], base=0, channel_multiplier=0, allow_small_or_imprecise_dtypes=True)
            nc.gpsimd.iota(floor_c[:], [[1, 1]], base=-FN, channel_multiplier=FN, allow_small_or_imprecise_dtypes=True)
            pool.wait_ge(ident_zeroed, 1)
            nc.gpsimd.affine_select(out=ident[:], in_=ident[:], compare_op=ALU.not_equal, fill=1.0, base=0,
                                    pattern=[[-1, P]], channel_multiplier=1).then_inc(consts_ready, 1)

            def normalise(i, par, first):
                pool.wait_ge(shift_ready[par], i + 1)
                if not first:
                    pool.wait_ge(xT_ready[par], i)
                k = ACT_FROM - POOL_FROM
                xr = acc[:, bass.ds((i * 2 + par) * (NB * D) + POOL_FROM * D, k * D)].rearrange("p (n f) -> p n f", f=D)
                y = xn[par][:, POOL_FROM * D:ACT_FROM * D].rearrange("p (n f) -> p n f", f=D)
                scale, offset = (v[:, par, POOL_FROM:ACT_FROM].unsqueeze(2).to_broadcast([P, k, D]) for v in (rstd, shift))
                nc.gpsimd.tensor_tensor(y, xr, scale, ALU.mult).then_inc(scaled[par], 1)
                pool.wait_ge(scaled[par], i + 1)
                nc.gpsimd.tensor_tensor(y, y, offset, ALU.add).then_inc(xn_pool_ready[par], 1)

            for par in range(2):
                normalise(0, par, True)
            with pool.Fori(1, BATCHES // 2) as i:
                for par in range(2):
                    normalise(i, par, False)
            for par in range(2):
                pool.wait_ge(p_stored[par], BATCHES // 2 * 16)

            arrived_reg = pool.alloc_register("indices_arrived")

            def chunk(c):
                arrived = c * 16 + 16
                if not isinstance(c, int):
                    pool.reg_add(arrived_reg, c * 16, 16)
                    arrived = arrived_reg
                for s in range(G):
                    pool.wait_ge(p_stored[1], BATCHES // 2 * 16)
                    pool.wait_ge(idx_in[s], arrived)
                    wait(pool, seg_ready[s], c)
                    for t in range(T):
                        pool.indirect_dma_start(
                            out=rows[:, s, t, :], out_offset=None, in_=p_rows[:, :],
                            in_offset=bass.IndirectOffsetOnAxis(ap=idx[:, s, t:t + 1], axis=0)).then_inc(rows_in[s], 16)

            chunk(0)

            def general():
                for s in range(G):
                    pool.wait_ge(rows_in[s], 16 * T)
                nc.gpsimd.memset(g_zero, 0.0).then_inc(g_zeroed, 1)
                nc.gpsimd.memset(g_one, 1.0).then_inc(g_zeroed, 1)
                nc.gpsimd.memset(g_earlier, 1.0).then_inc(g_zeroed, 1)
                pool.wait_ge(g_zeroed, 3)
                nc.gpsimd.affine_select(out=g_earlier, in_=g_earlier, compare_op=ALU.is_gt, fill=0.0, base=0,
                                        pattern=[[-1, P]], channel_multiplier=1).then_inc(g_mask_set, 1)
                pool.wait_ge(g_q_stored, NT * 16)
                pool.dma_start(sum_rows.rearrange("(n p) f -> p n f", p=P),
                               g_zero.unsqueeze(1).to_broadcast([P, NT, ROW])).then_inc(g_scattered, 16)
                arrived = pool.alloc_register("tile_arrived")
                with pool.Fori(0, TILES) as t:
                    pool.reg_add(arrived, t * 16, 16)
                    pool.wait_ge(p_stored[1], BATCHES // 2 * 16)
                    pool.wait_ge(g_src_in, arrived)
                    pool.wait_ge(g_dst_in, arrived)
                    pool.wait_ge(g_scattered, arrived)
                    for gathered, (buffer, table, index) in zip(g_gathered, ((g_p, p_rows, g_src), (g_q, q_rows, g_dst), (g_sum, sum_rows, g_dst))):
                        pool.indirect_dma_start(out=buffer, out_offset=None, in_=table[:, :],
                                                in_offset=bass.IndirectOffsetOnAxis(ap=index, axis=0)).then_inc(gathered, 16)
                    pool.reg_add(arrived, t, 1)
                    pool.wait_ge(flag_ready, 1)
                    pool.wait_ge(g_new_ready, arrived)
                    pool.indirect_dma_start(out=sum_rows[:, :], out_offset=bass.IndirectOffsetOnAxis(ap=g_out_idx, axis=0),
                                            in_=g_new, in_offset=None, bounds_check=NPAD - 1,
                                            oob_is_err=False).then_inc(g_scattered, 16)
            choose(pool, lambda: over_chunks(pool, chunk, 1), general)

        @block.scalar
        def _(act):
            act.dma_start(b2_col[:], b2.unsqueeze(1)).then_inc(bias_in, 16)
            act.dma_start(bih_col[:], b_ih).then_inc(bias_in, 16)
            act.dma_start(bhh_col[:], b_hh).then_inc(bias_in, 16)
            act.wait_ge(eps_set, 1)
            nc.scalar.activation(table_load[:], eps_col[:], ACT.Sqrt)

            def deviation(i, par):
                act.wait_ge(aggr_done[par], i + 1)
                nc.scalar.activation(std[:, par, :], mv[:, par, :, 1], ACT.Sqrt, bias=eps_col[:]).then_inc(std_ready[par], 1)

            def normalise(i, par, first):
                act.wait_ge(shift_ready[par], i + 1)
                if not first:
                    act.wait_ge(xT_ready[par], i)
                for t in range(ACT_FROM, NB):
                    last = nc.scalar.activation(xn[par][:, t * D:(t + 1) * D],
                                                acc[:, bass.ds((i * 2 + par) * (NB * D) + t * D, D)], ACT.Identity,
                                                bias=shift[:, par, t:t + 1], scale=rstd[:, par, t:t + 1])
                last.then_inc(xn_act_ready[par], 1)

            def relu_tiles(i, par, first):
                act.wait_ge(xT_ready[par], i + 1)
                if not first:
                    act.wait_ge(p_ready[par], i)
                nc.scalar.activation(hT_batch[par], xT_ps[par], ACT.Relu).then_inc(hT_ready[par], 1)
                nc.scalar.activation(hT[:, bass.ds((i * 2 + par) * (NB * D), NB * D)], xT_ps[par], ACT.Relu).then_inc(hT_kept[par], 1)

            def copy_products(i, par, first):
                act.wait_ge(p_ready[par], i + 1)
                if not first:
                    act.wait_ge(p_stored[par], i * 16)
                nc.scalar.copy(stage[par].rearrange("p n f -> p (n f)"), p_ps[par]).then_inc(p_copied[par], 1)

            def turn(i, first):
                deviation(i, 1)
                normalise(i, 0, False)
                relu_tiles(i - 1, 1, first)
                copy_products(i - 1, 0, first)
                deviation(i + 1, 0)
                normalise(i, 1, False)
                relu_tiles(i, 0, False)
                copy_products(i - 1, 1, first)

            deviation(0, 0)
            deviation(0, 1)
            normalise(0, 0, True)
            deviation(1, 0)
            normalise(0, 1, True)
            relu_tiles(0, 0, True)
            turn(1, True)
            with act.Fori(2, BATCHES // 2 - 1) as i:
                turn(i, False)
            i = BATCHES // 2 - 1
            deviation(i, 1)
            normalise(i, 0, False)
            relu_tiles(i - 1, 1, False)
            copy_products(i - 1, 0, False)
            normalise(i, 1, False)
            relu_tiles(i, 0, False)
            copy_products(i - 1, 1, False)
            relu_tiles(i, 1, False)
            copy_products(i, 0, False)
            copy_products(i, 1, False)

            act.wait_ge(w2T_ready, 1)
            nc.scalar.copy(w2T, setup_ps[:, 0:D]).then_inc(w2T_copied, 1)
            act.wait_ge(w2ih_ready, 1)
            nc.scalar.copy(w2ih[:], setup_ps[:, 0:GATES]).then_inc(w2ih_copied, 1)
            act.wait_ge(w2ih_ready, 2)
            nc.scalar.copy(b2ih[:], setup_ps[0:1, 0:GATES]).then_inc(w2ih_copied, 1)
            act.wait_ge(ranges_ready, 1)
            act.dma_start(base_f_dram, base_f[0:CHUNKS, :]).then_inc(base_stored, 16)
            act.dma_start(base_i_dram, base_n[0:CHUNKS, :]).then_inc(base_stored, 16)
            act.wait_ge(base_stored, 32)
            act.dma_start(base_i, base_i_dram.rearrange("(o c) g -> o (c g)", o=1)).then_inc(base_i_in, 16)
            act.dma_start(base_bc, base_f_dram.rearrange("(o c) g -> o (c g)", o=1).to_broadcast([P, GROUPS])).then_inc(base_bc_in, 16)
            act.wait_ge(consts_ready, 1)
            nc.scalar.copy(acc[:, N_ZERO_DVE:N], zero_col[:].to_broadcast([P, N - N_ZERO_DVE])).then_inc(acc_zeroed, 1)

            act.wait_ge(base_i_in, 16)
            for par in range(2):
                act.wait_ge(hT_kept[par], BATCHES // 2)

            def copy_window(c, s):
                b = act.value_load(base_i[0:1, bass.ds(c * G + s, 1)], min_val=0, max_val=BMAX)
                old = before(c, s, 1)
                if old:
                    act.wait_ge(onehotT_ready[old[1]], old[0] + 1)
                nc.scalar.copy(h_win[:], hT[:, bass.ds(b, W)]).then_inc(h_win_ready[s], 1)

            def copy_onehot(c, s):
                act.wait_ge(onehotT_ready[s], c + 1)
                wait(act, pre_ready[s], c)
                nc.scalar.activation(lhs[0:WB, s, :], onehotT_ps, ACT.Copy, accum_out=count[:, s:s + 1])
                nc.scalar.copy(rhs[0:W, s, :], q_ps).then_inc(lhs_ready[s], 1)

            def relu_message(c, s):
                act.wait_ge(summed[s], c + 1)
                m = rows[:, s, :, :]
                nc.scalar.activation(m, m, ACT.Relu).then_inc(message_ready[s], 1)

            def load_x_fin(n):
                wait(act, out_ready, n)
                act.dma_start(x_fin[:], x[bass.ds(n * FN, FN), :]).then_inc(x_fin_in, 16)

            def gate_activations(n):
                act.wait_ge(gates_ready, n + 1)
                wait(act, upd_ready, n)
                for g in range(2):
                    last = nc.scalar.activation(rz[:, g, :], gate_ps[:, g, :], ACT.Sigmoid, bias=brz_col[:, g:g + 1])
                last.then_inc(rz_ready, 1)

            def candidate(n):
                act.wait_ge(n_pre_ready, n + 1)
                nc.scalar.activation(cand[:], cand[:], ACT.Tanh, bias=bih_col[:, 2:3]).then_inc(cand_ready, 1)

            def store(n):
                act.wait_ge(out_ready, n + 1)
                act.dma_start(out[bass.ds(n * FN, FN), :], out_fin[:]).then_inc(stored, 16)

            def chunk(c):
                n, ending = finishing(c)
                for s in range(G):
                    if s == 0:
                        copy_window(c, 0)
                    copy_onehot(c, s)
                    if s + 1 < G:
                        copy_window(c, s + 1)
                    old = before(c, s, 2)
                    if old:
                        relu_message(*old)
                    if s == 1 and ending is not None:
                        store(ending)
                    if s == 2 and n is not None:
                        load_x_fin(n)
                    if s == 3 and n is not None:
                        gate_activations(n)
                    if s == 4 and n is not None:
                        candidate(n)

            def fin(n):
                load_x_fin(n)
                gate_activations(n)
                candidate(n)
                store(n)

            def finish_last():
                n = CHUNKS - LAG
                act.wait_ge(seg_ready[1], CHUNKS)
                act.dma_start(last_x, x[N - LN:N, :].rearrange("(k p) f -> p k f", p=FN)).then_inc(x_fin_in, 16)
                for g in range(2):
                    act.wait_ge(gates_ready, n + 1 + g)
                    nc.scalar.activation(last_rz[:, g, :], last_ps[g], ACT.Sigmoid, bias=brz_col[:, g:g + 1]).then_inc(rz_ready, 1)
                act.wait_ge(n_pre_ready, n + 1)
                nc.scalar.activation(last_cand, last_cand, ACT.Tanh, bias=bih_col[:, 2:3]).then_inc(cand_ready, 1)
                act.wait_ge(out_ready, n + 1)
                act.dma_start(out[N - LN:N, :].rearrange("(k p) f -> p k f", p=FN), last_out).then_inc(stored, 16)
                act.wait_ge(stored, (n + 1) * 16)

            def fast():
                over_chunks(act, chunk)
                for back in (2, 1):
                    relu_message(CHUNKS - 1, G - back)
                store(CHUNKS - LAG - 1)
                finish_last()

            def general():
                for s in range(G):
                    act.wait_ge(rows_in[s], 16 * T)

                def q_tile(j):
                    wait(act, g_q_ready, j)
                    nc.scalar.copy(g_bc, hT[:, bass.ds(j * P, P)]).then_inc(g_h_ready, 1)
                    wait(act, g_q_stored, j * 16)
                    act.wait_ge(g_q_ready, j + 1)
                    nc.scalar.copy(g_q, seg_ps[:, 0:D]).then_inc(g_q_copied, 1)
                q_tile(0)
                with act.Fori(1, NT) as j:
                    q_tile(j)
                with act.Fori(0, TILES) as t:
                    act.wait_ge(g_summed, t + 1)
                    nc.scalar.activation(g_p, g_p, ACT.Relu).then_inc(g_message_ready, 1)
                with act.Fori(0, NT) as j:
                    act.wait_ge(g_sumsT_ready, j + 1)
                    nc.scalar.copy(acc[:, bass.ds(j * P, P)], seg_ps[:, 0:P])
                    nc.scalar.copy(deg[0:1, bass.ds(j * P, P)], gate_ps1[0:1, 0:P]).then_inc(g_sumsT_kept, 1)
                over_fin(act, fin)
                act.wait_ge(stored, CHUNKS * 16)
            choose(act, fast, general)

        @block.vector
        def _(dve):
            chain = [0]

            def link(ins):
                chain[0] += 1
                ins.then_inc(dve_chain, 1)
                dve.wait_ge(dve_chain, chain[0])

            nc.vector.memset(eps_col[:], EPS).then_inc(eps_set, 1)
            turn_reg = dve.alloc_register("turn")

            def statistics(i, par, first):
                turn = 1
                if not first:
                    dve.reg_add(turn_reg, i, 1)
                    turn = turn_reg
                dve.wait_ge(x_in[par], i * 16 + 16)
                for t in range(NB):
                    last = nc.vector.bn_stats(stats[:, par, t, :], acc[:, bass.ds((i * 2 + par) * (NB * D) + t * D, D)])
                last.then_inc(stats_done[par], 1)
                dve.wait_ge(eps_set, 1)
                dve.wait_ge(stats_done[par], turn)
                for t in range(NB):
                    last = nc.vector.bn_aggr(mv[:, par, t, :], stats[:, par, t, :])
                last.then_inc(aggr_done[par], 1)

            def scales(i, par, first):
                if not first:
                    dve.wait_ge(xn_pool_ready[par], i)
                dve.wait_ge(std_ready[par], i + 1)
                nc.vector.reciprocal(rstd[:, par, :], std[:, par, :]).then_inc(rstd_done[par], 1)
                dve.wait_ge(rstd_done[par], i + 1)
                nc.vector.scalar_tensor_tensor(out=shift[:, par, :], in0=mv[:, par, :, 0], scalar=-1.0, in1=rstd[:, par, :],
                                               op0=ALU.mult, op1=ALU.mult).then_inc(shift_ready[par], 1)

            def normalise(i, par, first):
                if not first:
                    dve.wait_ge(xT_ready[par], i)
                for t in range(POOL_FROM):
                    last = nc.vector.tensor_scalar(xn[par][:, t * D:(t + 1) * D],
                                                   acc[:, bass.ds((i * 2 + par) * (NB * D) + t * D, D)],
                                                   mv[:, par, t, 0:1], rstd[:, par, t:t + 1], ALU.subtract, ALU.mult)
                last.then_inc(xn_dve_ready[par], 1)

            statistics(0, 0, True)
            scales(0, 0, True)
            statistics(0, 1, True)
            normalise(0, 0, True)
            scales(0, 1, True)
            statistics(1, 0, False)
            normalise(0, 1, True)
            scales(1, 0, False)
            with dve.Fori(1, BATCHES // 2 - 1) as i:
                statistics(i, 1, False)
                normalise(i, 0, False)
                scales(i, 1, False)
                statistics(i + 1, 0, False)
                normalise(i, 1, False)
                scales(i + 1, 0, False)
            i = BATCHES // 2 - 1
            dve.wait_ge(x_tail_in, 16)
            statistics(i, 1, False)
            normalise(i, 0, False)
            scales(i, 1, False)
            normalise(i, 1, False)

            dve.wait_ge(dstn_in, 16)
            dn = dst_nat.rearrange("c (g e) -> c g e", g=G)
            nc.vector.tensor_reduce(gmin[0:CHUNKS, :], dn, AX.X, ALU.min)
            link(nc.vector.tensor_reduce(gmax[0:CHUNKS, :], dn, AX.X, ALU.max))
            link(nc.vector.tensor_scalar(base_f[0:CHUNKS, :], gmin[0:CHUNKS, :], float(BMAX), None, ALU.min))
            nc.vector.tensor_copy(base_n[0:CHUNKS, :], base_f[0:CHUNKS, :]).then_inc(ranges_ready, 1)
            link(nc.vector.tensor_tensor(gmax[0:CHUNKS, :], gmax[0:CHUNKS, :], base_f[0:CHUNKS, :], ALU.subtract))
            nc.vector.tensor_reduce(viol[0:CHUNKS, 0:1], gmax[0:CHUNKS, :], AX.X, ALU.max)
            link(nc.vector.tensor_reduce(viol[0:CHUNKS, 1:2], gmin[0:CHUNKS, :], AX.X, ALU.min))
            nc.vector.tensor_scalar(viol[0:CHUNKS, 0:1], viol[0:CHUNKS, 0:1], float(W - 1), None, ALU.subtract)
            dve.wait_ge(consts_ready, 1)
            link(nc.vector.tensor_tensor(viol[0:CHUNKS, 1:2], floor_c[0:CHUNKS, :], viol[0:CHUNKS, 1:2], ALU.subtract))
            nc.vector.tensor_tensor(viol[0:CHUNKS, 2:3], viol[0:CHUNKS, 0:1], viol[0:CHUNKS, 1:2], ALU.max).then_inc(viol_ready, 1)
            for par in range(2):
                dve.wait_ge(xT_ready[par], BATCHES // 2)
            nc.vector.memset(acc[:, 0:N_ZERO_DVE], 0.0).then_inc(acc_zeroed, 1)

            dve.wait_ge(bias_in, 48)
            nc.vector.tensor_tensor(brz_col[:], bih_col[:, 0:2], bhh_col[:, 0:2], ALU.add)
            dve.wait_ge(base_bc_in, 16)
            dve.wait_ge(base_i_in, 16)
            dve.wait_ge(dst_in, 16 * DST_PARTS)
            dr = dst_rel.rearrange("p (g t) -> p g t", t=T)
            nc.vector.tensor_tensor(dr, dst_int[:, :].rearrange("p (g t) -> p g t", t=T),
                                    base_bc.unsqueeze(2).to_broadcast([P, GROUPS, T]), ALU.subtract).then_inc(dst_rel_ready, 1)
            dve.wait_ge(dst_rel_ready, 1)
            nc.vector.memset(onehot[:, :, :, W:WB], 1.0).then_inc(ones_set, 1)
            dve.wait_ge(ones_set, 1)

            def build_onehot(c, s):
                wait(dve, seg_ready[s], c)
                d = dst_rel[:, bass.ds(c * (G * T) + s * T, T)]
                nc.vector.tensor_tensor(onehot[:, s, :, 0:W], iota_w[:, :].unsqueeze(1).to_broadcast([P, T, W]),
                                        d.unsqueeze(2).to_broadcast([P, T, W]), ALU.is_equal).then_inc(onehot_ready[s], 1)

            def add_pre(c, s):
                dve.wait_ge(pre_ready[s], c + 1)
                dve.wait_ge(rows_in[s], c * (16 * T) + 16 * T)
                r = rows[:, s, :, :].rearrange("p t f -> p (t f)")
                nc.vector.tensor_tensor(r, r, pre_ps[s % 2], ALU.add).then_inc(summed[s], 1)

            def add_segments(c, s, prev):
                b = dve.value_load(base_i[0:1, bass.ds(c * G + s, 1)], min_val=0, max_val=BMAX)
                dve.wait_ge(seg_ready[s], c + 1)
                if prev:
                    dve.wait_ge(acc_added[prev[1]], prev[0] * 2 + 2)
                sg = seg_ps
                nc.vector.tensor_tensor(acc[:, bass.ds(b, W)], acc[:, bass.ds(b, W)], sg[:, 0:W], ALU.add).then_inc(acc_added[s], 1)
                nc.vector.tensor_tensor(deg[0:1, bass.ds(b, W)], deg[0:1, bass.ds(b, W)], sg[0:1, W:2 * W],
                                        ALU.add).then_inc(acc_added[s], 1)

            def candidate_pre(n):
                dve.wait_ge(rz_ready, n + 1)
                nc.vector.scalar_tensor_tensor(out=upd[:], in0=gate_ps[:, 3, :], scalar=bhh_col[:, 2:3], in1=rz[:, 0, :],
                                               op0=ALU.add, op1=ALU.mult).then_inc(fin_chain, 1)
                dve.wait_ge(fin_chain, n * 3 + 1)
                nc.vector.tensor_tensor(cand[:], upd[:], gate_ps[:, 2, :], ALU.add).then_inc(n_pre_ready, 1)

            def update(n):
                dve.wait_ge(cand_ready, n + 1)
                h = hT[:, bass.ds(n * FN, FN)]
                nc.vector.tensor_tensor(upd[:], h, cand[:], ALU.subtract).then_inc(fin_chain, 1)
                dve.wait_ge(fin_chain, n * 3 + 2)
                nc.vector.tensor_tensor(upd[:], upd[:], rz[:, 1, :], ALU.mult).then_inc(fin_chain, 1)
                dve.wait_ge(fin_chain, n * 3 + 3)
                nc.vector.tensor_tensor(upd[:], upd[:], cand[:], ALU.add).then_inc(upd_ready, 1)

            def residual(n):
                dve.wait_ge(back_ready, n + 1)
                dve.wait_ge(x_fin_in, n * 16 + 16)
                wait(dve, stored, n * 16)
                nc.vector.tensor_tensor(out_fin[:], x_fin[:], back_ps, ALU.add).then_inc(out_ready, 1)

            def chunk(c):
                n, ending = finishing(c)
                for s in range(G):
                    build_onehot(c, s)
                    old = before(c, s, 2)
                    if old:
                        add_pre(*old)
                    old = before(c, s, 3)
                    if old:
                        if isinstance(c, int) and c == 0 and s == 3:
                            dve.wait_ge(deg_zeroed, 16)
                        add_segments(*old, before(c, s, 4))
                    if s == 0 and ending is not None:
                        residual(ending)
                    if s == 3 and n is not None:
                        candidate_pre(n)
                    if s == 4 and n is not None:
                        update(n)

            def fin(n):
                candidate_pre(n)
                update(n)
                residual(n)

            def finish_last():
                n = CHUNKS - LAG
                dve.wait_ge(rz_ready, n + 1)
                nc.vector.scalar_tensor_tensor(out=last_upd, in0=last_ps[3], scalar=bhh_col[:, 2:3], in1=last_rz[:, 0, :],
                                               op0=ALU.add, op1=ALU.mult).then_inc(fin_chain, 1)
                dve.wait_ge(fin_chain, n * 3 + 1)
                nc.vector.tensor_tensor(last_cand, last_upd, last_ps[2], ALU.add).then_inc(n_pre_ready, 1)
                dve.wait_ge(cand_ready, n + 1)
                nc.vector.tensor_tensor(last_upd, hT[:, N - LN:N], last_cand, ALU.subtract).then_inc(fin_chain, 1)
                dve.wait_ge(rz_ready, n + 2)
                dve.wait_ge(fin_chain, n * 3 + 2)
                nc.vector.tensor_tensor(last_upd, last_upd, last_rz[:, 1, :], ALU.mult).then_inc(fin_chain, 1)
                dve.wait_ge(fin_chain, n * 3 + 3)
                nc.vector.tensor_tensor(last_upd, last_upd, last_cand, ALU.add).then_inc(upd_ready, 1)
                dve.wait_ge(x_fin_in, n * 16 + 16)
                dve.wait_ge(back_ready, n + 1)
                nc.vector.tensor_tensor(last_out, last_x, last_back, ALU.add).then_inc(out_ready, 1)

            def fast():
                over_chunks(dve, chunk)
                residual(CHUNKS - LAG - 1)
                c = CHUNKS - 1
                add_pre(c, G - 2)
                add_segments(c, G - 3, (c, G - 4))
                add_pre(c, G - 1)
                add_segments(c, G - 2, (c, G - 3))
                add_segments(c, G - 1, (c, G - 2))
                finish_last()

            def general():
                dve.wait_ge(g_mask_set, 1)
                dve.wait_ge(g_q_stored, NT * 16)
                nc.vector.memset(g_new, 0.0)
                with dve.Fori(0, TILES) as t:
                    step = [0]
                    steps = 8

                    def then(ins):
                        step[0] += 1
                        ins.then_inc(g_chain, 1)
                        dve.wait_ge(g_chain, t * steps + step[0])

                    dve.wait_ge(g_dst_in, t * 16 + 16)
                    then(nc.vector.tensor_copy(g_dstf, g_dst))
                    nc.vector.tensor_copy(g_bc, g_dstf.to_broadcast([P, P])).then_inc(g_bc_ready, 1)
                    dve.wait_ge(g_bcT_ready, t + 1)
                    then(nc.vector.tensor_scalar(g_eq, g_dst_ps, g_dstf, None, ALU.is_equal))
                    then(nc.vector.tensor_reduce(g_count, g_eq, AX.X, ALU.add))
                    then(nc.vector.tensor_tensor(g_dup, g_eq, g_earlier, ALU.mult))
                    then(nc.vector.tensor_reduce(g_isdup, g_dup, AX.X, ALU.max))
                    then(nc.vector.scalar_tensor_tensor(out=g_outf, in0=g_isdup, scalar=float(2 * NPAD), in1=g_dstf,
                                                        op0=ALU.mult, op1=ALU.add))
                    then(nc.vector.tensor_copy(g_out_idx, g_outf))
                    dve.wait_ge(g_pre_ready, t + 1)
                    for gathered in g_gathered:
                        dve.wait_ge(gathered, t * 16 + 16)
                    then(nc.vector.tensor_tensor(g_p, g_p, pre_ps[0][:, 0:D], ALU.add))
                    assert step[0] == steps
                    nc.vector.tensor_tensor(g_p, g_p, g_q, ALU.add).then_inc(g_summed, 1)
                    nc.vector.tensor_tensor(g_new[:, D:D + 1], g_sum[:, D:D + 1], g_count, ALU.add)
                    dve.wait_ge(g_seg_ready, t + 1)
                    nc.vector.tensor_tensor(g_new[:, 0:D], g_sum[:, 0:D], seg_ps[:, 0:D], ALU.add).then_inc(g_new_ready, 1)
                over_fin(dve, fin)

            dve.wait_ge(violT_ready, 1)
            link(nc.vector.tensor_reduce(flag_f[:], violT_ps, AX.X, ALU.max))
            nc.vector.tensor_scalar(flag_i[:], flag_f[:], 0.0, None, ALU.is_gt).then_inc(flag_ready, 1)
            choose(dve, fast, general)

        @block.tensor
        def _(pe):
            pe.wait_ge(consts_ready, 1)
            pe.wait_ge(w1_in, 16)

            def transpose_rows(i, par, first):
                pe.wait_ge(xn_dve_ready[par], i + 1)
                pe.wait_ge(xn_pool_ready[par], i + 1)
                pe.wait_ge(xn_act_ready[par], i + 1)
                if not first:
                    pe.wait_ge(hT_kept[par], i)
                for t in range(NB):
                    last = nc.tensor.transpose(xT_ps[par][:, t * D:(t + 1) * D], xn[par][:, t * D:(t + 1) * D], ident[:])
                last.then_inc(xT_ready[par], 1)

            def products(i, par, first):
                pe.wait_ge(hT_ready[par], i + 1)
                if not first:
                    pe.wait_ge(p_copied[par], i)
                for t in range(NB):
                    last = nc.tensor.matmul(p_ps[par][:, t * D:(t + 1) * D], hT_batch[par][:, t * D:(t + 1) * D], w1_src,
                                            start=True, stop=True)
                last.then_inc(p_ready[par], 1)

            transpose_rows(0, 0, True)
            transpose_rows(0, 1, True)
            products(0, 0, True)
            transpose_rows(1, 0, False)
            products(0, 1, True)
            with pe.Fori(1, BATCHES // 2 - 1) as i:
                transpose_rows(i, 1, False)
                products(i, 0, False)
                transpose_rows(i + 1, 0, False)
                products(i, 1, False)
            i = BATCHES // 2 - 1
            transpose_rows(i, 1, False)
            products(i, 0, False)
            products(i, 1, False)

            for par in range(2):
                pe.wait_ge(hT_kept[par], BATCHES // 2)
                pe.wait_ge(p_copied[par], BATCHES // 2)
            pe.wait_ge(weights_in, 16 * 6)
            nc.tensor.transpose(setup_ps[:, 0:D], w2_sb, ident[:]).then_inc(w2T_ready, 1)
            pe.wait_ge(w2T_copied, 1)
            nc.tensor.matmul(setup_ps[:, 0:GATES], w2T, wih_sb, start=True, stop=True).then_inc(w2ih_ready, 1)
            pe.wait_ge(w2ih_copied, 1)
            pe.wait_ge(bias_in, 48)
            nc.tensor.matmul(setup_ps[0:1, 0:GATES], b2_col[:], wih_sb, start=True, stop=True).then_inc(w2ih_ready, 1)
            pe.wait_ge(w2ih_copied, 2)
            pe.wait_ge(viol_ready, 1)
            nc.tensor.transpose(violT_ps, viol[0:CHUNKS, 2:3], ident[0:CHUNKS, 0:CHUNKS]).then_inc(violT_ready, 1)

            def transpose_onehot(c, s):
                pe.wait_ge(onehot_ready[s], c + 1)
                old = before(c, s, 1)
                if old:
                    pe.wait_ge(lhs_ready[old[1]], old[0] + 1)
                for t in range(T):
                    nc.tensor.transpose(onehotT_ps[:, t * P:(t + 1) * P], onehot[:, s, t, :], ident[:])
                pe.wait_ge(h_win_ready[s], c + 1)
                nc.tensor.matmul(q_ps, h_win[:], w1_dst[:], start=True, stop=True).then_inc(onehotT_ready[s], 1)

            def pre_activation(c, s):
                old = before(c, s, {0: 1, 1: 3}.get(s, 2))
                if old:
                    pe.wait_ge(summed[old[1]], old[0] + 1)
                pe.wait_ge(lhs_ready[s], c + 1)
                pe.wait_ge(ea_in[s], c * 16 + 16)
                for t in range(T):
                    last = nc.tensor.matmul(pre_ps[s % 2][:, t * D:(t + 1) * D], lhs[:, s, t * P:(t + 1) * P],
                                            rhs[:, s, :], start=True, stop=True)
                last.then_inc(pre_ready[s], 1)

            def segment_sums(c, s):
                pe.wait_ge(message_ready[s], c + 1)
                old = before(c, s, 1)
                if old:
                    pe.wait_ge(acc_added[old[1]], old[0] * 2 + 2)
                sg = seg_ps
                for t in range(T):
                    nc.tensor.matmul(sg[:, 0:W], rows[:, s, t, :], onehot[:, s, t, 0:W], start=(t == 0), stop=(t == T - 1))
                nc.tensor.transpose(sg[0:1, W:2 * W], count[0:W, s:s + 1], ident[0:W, 0:W]).then_inc(seg_ready[s], 1)

            def gates(n):
                if not (isinstance(n, int) and n == 0):
                    wait(pe, out_ready, n)
                a, d, h = (v[:, bass.ds(n * FN, FN)] for v in (acc, deg, hT))
                for g in range(3):
                    cols = slice(g * D, (g + 1) * D)
                    nc.tensor.matmul(gate_ps[:, g, :], w2ih[:, cols], a, start=True, stop=False)
                    last = nc.tensor.matmul(gate_ps[:, g, :], b2ih[0:1, cols], d, start=False, stop=(g == 2))
                    if g < 2:
                        nc.tensor.matmul(gate_ps[:, g, :], whh_sb[:, cols], h, start=False, stop=True)
                nc.tensor.matmul(gate_ps[:, 3, :], whh_sb[:, 2 * D:3 * D], h, start=True, stop=True).then_inc(gates_ready, 1)

            def back(n):
                pe.wait_ge(upd_ready, n + 1)
                nc.tensor.transpose(back_ps, upd[:], ident[:]).then_inc(back_ready, 1)

            def chunk(c):
                n, ending = finishing(c)
                for s in range(G):
                    transpose_onehot(c, s)
                    old = before(c, s, 1)
                    if old:
                        pre_activation(*old)
                    old = before(c, s, 2)
                    if old:
                        segment_sums(*old)
                    if s == 0 and ending is not None:
                        back(ending)
                    if s == 2 and n is not None:
                        pe.wait_ge(acc_added[G - 1], c * 2)
                        gates(n)

            def fin(n):
                gates(n)
                back(n)

            def fast():
                over_chunks(pe, chunk)
                back(CHUNKS - LAG - 1)
                c = CHUNKS - 1
                pre_activation(c, G - 1)
                segment_sums(c, G - 2)
                pe.wait_ge(lhs_ready[G - 1], CHUNKS)
                pe.wait_ge(summed[G - 2], CHUNKS)
                h = hT[:, N - LN:N]
                for g in range(2):
                    nc.tensor.matmul(last_ps[g], whh_sb[:, g * D:(g + 1) * D], h, start=True, stop=False)
                nc.tensor.matmul(last_ps[3], whh_sb[:, 2 * D:3 * D], h, start=True, stop=True)
                segment_sums(c, G - 1)
                pe.wait_ge(acc_added[G - 1], CHUNKS * 2)
                a, d = acc[:, N - LN:N], deg[0:1, N - LN:N]
                for g in (2, 0, 1):
                    cols = slice(g * D, (g + 1) * D)
                    nc.tensor.matmul(last_ps[g], w2ih[:, cols], a, start=(g == 2), stop=False)
                    last = nc.tensor.matmul(last_ps[g], b2ih[0:1, cols], d, start=False, stop=True)
                    if g < 2:
                        last.then_inc(gates_ready, 1)
                n = CHUNKS - LAG
                pe.wait_ge(out_ready, n)
                pe.wait_ge(upd_ready, n + 1)
                for k in range(LAG):
                    last = nc.tensor.transpose(last_back[:, k, :], last_upd[:, k * FN:(k + 1) * FN], ident[:])
                last.then_inc(back_ready, 1)

            def general():
                pe.wait_ge(g_zeroed, 3)
                pe.wait_ge(g_b1_in, 16)

                def q_tile(j):
                    pe.wait_ge(g_h_ready, j + 1)
                    wait(pe, g_q_copied, j)
                    nc.tensor.matmul(seg_ps[:, 0:D], g_bc, w1_dst[:], start=True, stop=False)
                    nc.tensor.matmul(seg_ps[:, 0:D], g_one, g_b1, start=False, stop=True).then_inc(g_q_ready, 1)
                q_tile(0)
                with pe.Fori(1, NT) as j:
                    q_tile(j)
                with pe.Fori(0, TILES) as t:
                    pe.wait_ge(g_bc_ready, t + 1)
                    nc.tensor.transpose(g_dst_ps, g_bc, ident[:]).then_inc(g_bcT_ready, 1)
                    pe.wait_ge(g_ea_in, t * 16 + 16)
                    nc.tensor.matmul(pre_ps[0][:, 0:D], lhs[WB:P, 0, 0:P], rhs[WB:P, 0, :], start=True,
                                     stop=True).then_inc(g_pre_ready, 1)
                    pe.wait_ge(g_message_ready, t + 1)
                    nc.tensor.matmul(seg_ps[:, 0:D], g_eq, g_p, start=True, stop=True).then_inc(g_seg_ready, 1)

                def transpose_sums(j):
                    pe.wait_ge(g_sums_in, j * 16 + 16)
                    wait(pe, g_sumsT_kept, j)
                    nc.tensor.transpose(seg_ps[:, 0:P], g_sum[:, 0:D], ident[:])
                    nc.tensor.transpose(gate_ps1, g_sum[:, D:D + 1], ident[:]).then_inc(g_sumsT_ready, 1)
                transpose_sums(0)
                with pe.Fori(1, NT) as j:
                    transpose_sums(j)
                pe.wait_ge(g_sumsT_kept, NT)
                over_fin(pe, fin)
            choose(pe, fast, general)


_OUTS = [((N, D), "float32")]


def kernel(**inputs):
    import numpy as _np
    import concourse.bacc as _bacc
    from concourse import mybir as _mybir
    from concourse.bass_utils import run_bass_kernel_spmd as _run

    src = _np.asarray(inputs["src"])
    dst = _np.asarray(inputs["dst"])
    w = {k: _np.ascontiguousarray(inputs["L0_gnn_" + k]) for k in ("w1", "b1", "w2", "b2", "w_ih", "b_ih", "w_hh", "b_hh")}
    for k in ("b_ih", "b_hh"):
        w[k] = _np.ascontiguousarray(w[k].reshape(3, D).T)
    laid = {
        "x": _np.ascontiguousarray(inputs["x"]),
        "src_cols": _np.ascontiguousarray(src.reshape(GROUPS, T, P).transpose(0, 2, 1).reshape(GROUPS * P, T)),
        "dst_cols": _np.ascontiguousarray(dst.reshape(GROUPS * T, P).T),
        "dst_rows": _np.ascontiguousarray(dst.reshape(CHUNKS, G * GE)),
        "src_tiles": _np.ascontiguousarray(src.reshape(TILES, P)),
        "dst_tiles": _np.ascontiguousarray(dst.reshape(TILES, P)),
        "ea_t": _np.ascontiguousarray(_np.asarray(inputs["edge_attr_32"]).T),
        **w,
    }
    nc = _bacc.Bacc("TRN2", target_bir_lowering=False, num_devices=1)
    arrays, args = {}, []
    for name, a in laid.items():
        arrays[f"in_{name}_dram"] = a
        args.append(nc.dram_tensor(f"in_{name}_dram", a.shape, _mybir.dt.from_np(a.dtype), kind="ExternalInput").ap())
    for i, (shape, dtype) in enumerate(_OUTS):
        dt = _mybir.dt.from_np(_np.dtype(dtype))
        args.append(nc.dram_tensor(f"out_{i}_dram", shape, dt, kind="ExternalOutput").ap())
    gnn_kernel(nc, *args)
    r = _run(nc, [arrays], core_ids=[0])
    return r.results[0]["out_0_dram"]
```
